# Optimizing a Trainium2 kernel written in Bass

```python
import numpy as np
import jax
import jax.numpy as jnp

def _softmax(x, axis=-1):
    return jax.nn.softmax(x, axis=axis)

def _gelu(x):
    return jax.nn.gelu(x, approximate=True)

def _silu(x):
    return jax.nn.silu(x)

def _sigmoid(x):
    return jax.nn.sigmoid(x)

def _layernorm(x, axis=-1, eps=1e-05):
    m = jnp.mean(x, axis=axis, keepdims=True)
    v = jnp.var(x, axis=axis, keepdims=True)
    return (x - m) / jnp.sqrt(v + eps)

def _scatter_add(tgt, idx, src, axis=0):
    return tgt.at[idx].add(src)

def _segment_sum(src, seg, n):
    return jax.ops.segment_sum(src, seg, n)
kernel_name = 'mk_xattn_ffn_d4_seqx_r8_39cdc7'

def setup_inputs(seed: int=0):
    np.random.seed(seed)
    _w = jnp.asarray

    def _rec_inputs():
        import jax
        import jax.numpy as jnp
        _rk = jax.random.key(seed)
        x = -0.000125 + 0.9999 * jax.random.normal(jax.random.fold_in(_rk, 1), (8, 256, 128), jnp.float32)
        _lenS = 256 - jax.random.randint(jax.random.fold_in(_rk, 7), (8,), 0, max(1, 256 // 4) + 1, jnp.int32)
        _lenS2 = 256 - jax.random.randint(jax.random.fold_in(_rk, 8), (8,), 0, max(1, 256 // 4) + 1, jnp.int32)
        _ctx_2048P = jax.random.normal(jax.random.fold_in(_rk, 11), (8, 16, 256), jnp.float32)
        _ctx_2048c = jax.random.dirichlet(jax.random.fold_in(_rk, 511), 0.3 * jnp.ones((16,), jnp.float32), (8, 256))
        _ctx_2048t = jnp.einsum('bsk,bkd->bsd', _ctx_2048c, _ctx_2048P)
        _ctx_2048t = _ctx_2048t * jax.lax.rsqrt(jnp.mean(jnp.square(_ctx_2048t)) + 1e-12) * 0.953939
        ctx_2048 = -1.39393e-06 + 0.999914 * (_ctx_2048t + 0.3 * jax.random.normal(jax.random.fold_in(_rk, 611), (8, 256, 256), jnp.float32))
        _validS = jnp.arange(256)[None, :] < _lenS[:, None]
        _validS2 = jnp.arange(256)[None, :] < _lenS2[:, None]
        _causal = jnp.tril(jnp.ones((256, 256), dtype=bool))
        mask_BxS2_if0 = jnp.where(jnp.ones((8, 256), dtype=bool), 4, 0).astype(jnp.int32)
        mask_BxS2_fk1 = jnp.where(jnp.broadcast_to(_validS2[:, :], (8, 256)), 1.0, 0.0).astype(jnp.float32)
        return (x, ctx_2048, mask_BxS2_if0, mask_BxS2_fk1)
    x, ctx_2048, mask_BxS2_if0, mask_BxS2_fk1 = _rec_inputs()

    def _L0_xattn_setup():
        import jax, jax.numpy as jnp
        import numpy as np
        B, N, DIM = (8, 512, 128)
        M, CTX = (32, 256)
        HEADS, DH = (16, 64)
        INNER = HEADS * DH
        EPS = 1e-06

        def _split_heads(t):
            b, n, _ = t.shape
            return t.reshape(b, n, HEADS, DH).transpose(0, 2, 1, 3)
        key = jax.random.key(seed)
        ks = jax.random.split(key, 6)
        x = jax.random.normal(ks[0], (B, N, DIM), dtype=jnp.float32)
        context = jax.random.normal(ks[1], (B, M, CTX), dtype=jnp.float32)
        Wq = jax.random.normal(ks[2], (DIM, INNER), dtype=jnp.float32) / np.sqrt(DIM)
        Wkv = jax.random.normal(ks[3], (CTX, 2 * INNER), dtype=jnp.float32) / np.sqrt(CTX)
        null_kv = jax.random.normal(ks[4], (2, DH), dtype=jnp.float32) / np.sqrt(2.0)
        Wout = jax.random.normal(ks[5], (INNER, DIM), dtype=jnp.float32) / np.sqrt(INNER)
        ln_scale = jnp.ones((DIM,), dtype=jnp.float32)
        ln_bias = jnp.zeros((DIM,), dtype=jnp.float32)
        return {'x': x, 'context': context, 'Wq': Wq, 'Wkv': Wkv, 'null_kv': null_kv, 'Wout': Wout, 'ln_scale': ln_scale, 'ln_bias': ln_bias}
    _L0_xattn_all = _L0_xattn_setup()
    _L0_xattn_in = {k: v for k, v in _L0_xattn_all.items() if k in ('Wq', 'Wkv', 'null_kv', 'Wout', 'ln_scale', 'ln_bias')}
    del _L0_xattn_all

    def _L0_ffn_setup():
        import jax, jax.numpy as jnp
        import numpy as np
        DIM = 128

        def _reference_tuple_inner(x, W_r, W_k, W_v, mu_r, mu_k):
            B, T, C = x.shape
            x_prev = jnp.concatenate([jnp.zeros((B, 1, C), x.dtype), x[:, :-1, :]], axis=1)
            xr = mu_r * x + (1.0 - mu_r) * x_prev
            xk = mu_k * x + (1.0 - mu_k) * x_prev
            r = jax.nn.sigmoid(jnp.einsum('btc,dc->btd', xr, W_r))
            k = jnp.einsum('btc,dc->btd', xk, W_k)
            k_act = jnp.square(jax.nn.relu(k))
            out = r * jnp.einsum('btc,dc->btd', k_act, W_v)
            new_state = x[:, -1, :]
            return (out, new_state)
        key = jax.random.key(seed)
        ks = jax.random.split(key, 6)
        B, T, C = (8, 256, DIM)
        x = jax.random.normal(ks[0], (B, T, C), dtype=jnp.float32)
        s = 1.0 / np.sqrt(C)
        W_r = jax.random.uniform(ks[1], (C, C), jnp.float32, -s, s)
        W_k = jax.random.uniform(ks[2], (C, C), jnp.float32, -s, s)
        W_v = jax.random.uniform(ks[3], (C, C), jnp.float32, -s, s)
        mu_r = jax.random.uniform(ks[4], (C,), jnp.float32)
        mu_k = jax.random.uniform(ks[5], (C,), jnp.float32)
        return {'x': x, 'W_r': W_r, 'W_k': W_k, 'W_v': W_v, 'mu_r': mu_r, 'mu_k': mu_k}
    _L0_ffn_all = _L0_ffn_setup()
    _L0_ffn_in = {k: v for k, v in _L0_ffn_all.items() if k in ('W_r', 'W_k', 'W_v', 'mu_r', 'mu_k')}
    del _L0_ffn_all

    def _L1_xattn_setup():
        import jax, jax.numpy as jnp
        import numpy as np
        B, L, P = (4, 512, 128)
        D_MODEL = 128
        D_GLOBAL = 256
        HEADDIM = 32
        EPSILON = 0.001
        RMS_EPS = 1e-05

        def rmsnorm(x, g, eps=RMS_EPS):
            var = jnp.mean(jnp.square(x), axis=-1, keepdims=True)
            return x * jax.lax.rsqrt(var + eps) * g

        def _hnet_depool(h, h_patch_full, patch_lens):
            h_patch = h_patch_full[..., :D_MODEL]
            bsz, plen = (h_patch.shape[0], h_patch.shape[1])
            seqlen = h.shape[1]
            logp = jnp.full((bsz, plen), -EPSILON, dtype=jnp.float32)
            bidx = jnp.cumsum(patch_lens, axis=1) - 1
            boundary_mask = jnp.zeros((bsz, seqlen), dtype=jnp.int32)
            boundary_mask = boundary_mask.at[jnp.arange(bsz)[:, None], bidx].set(1)
            dt = (-jnp.log(-jnp.expm1(logp))).astype(h_patch.dtype)
            x = h_patch / dt[..., None]
            n_heads = D_MODEL // HEADDIM
            A = -jnp.ones((n_heads,), dtype=jnp.float32)
            bcoef = jnp.exp(logp).astype(h_patch.dtype)
            x4 = x.reshape(bsz, plen, n_heads, HEADDIM)
            a = jnp.exp(dt[:, :, None] * A[None, None, :])
            u = (dt * bcoef)[:, :, None, None] * x4
            a_b = jnp.broadcast_to(a[..., None], u.shape)

            def comb(lft, rgt):
                aL, uL = lft
                aR, uR = rgt
                return (aL * aR, uL * aR + uR)
            _, s = jax.lax.associative_scan(comb, (a_b, u), axis=1)
            depool = s.reshape(bsz, plen, D_MODEL)
            plug = jnp.clip(jnp.cumsum(boundary_mask, axis=1) - 1, 0, plen - 1)
            depool_out = depool[jnp.arange(bsz)[:, None], plug]
            return depool_out + h
        key = jax.random.key(seed)
        k1, k2, k3, k4 = jax.random.split(key, 4)
        embeds = jax.random.normal(k1, (B, L, D_MODEL), dtype=jnp.float32)
        patch_embeds = jax.random.normal(k2, (B, P, D_GLOBAL), dtype=jnp.float32)
        patch_lens = jnp.full((B, P), L // P, dtype=jnp.int64)
        W_in = jax.random.normal(k3, (D_MODEL, D_MODEL), dtype=jnp.float32) * 0.02
        b_in = jnp.zeros((D_MODEL,), dtype=jnp.float32)
        g_res = jnp.ones((D_MODEL,), dtype=jnp.float32)
        g_init = jnp.ones((D_GLOBAL,), dtype=jnp.float32)
        return {'embeds': embeds, 'patch_embeds': patch_embeds, 'patch_lens': patch_lens, 'W_in': W_in, 'b_in': b_in, 'g_res': g_res, 'g_init': g_init}
    _L1_xattn_all = _L1_xattn_setup()
    _L1_xattn_in = {k: v for k, v in _L1_xattn_all.items() if k in ('W_in', 'b_in', 'g_res', 'g_init')}
    del _L1_xattn_all

    def _L1_ffn_setup():
        import jax, jax.numpy as jnp
        import numpy as np
        D_MODEL = 128
        key = jax.random.key(seed)
        k_x, k_w, k_a1, k_a2 = jax.random.split(key, 4)
        x = jax.random.normal(k_x, (4, 256, D_MODEL), dtype=jnp.float32)
        weight = jax.random.normal(k_w, (D_MODEL, D_MODEL), dtype=jnp.float32) * 0.02
        aux_weight1 = jax.random.normal(k_a1, (D_MODEL, D_MODEL), dtype=jnp.float32) * 0.02
        aux_weight2 = jax.random.normal(k_a2, (D_MODEL, D_MODEL), dtype=jnp.float32) * 0.02
        bias = jnp.zeros((D_MODEL,), dtype=jnp.float32)
        return {'x': x, 'weight': weight, 'aux_weight1': aux_weight1, 'aux_weight2': aux_weight2, 'bias': bias}
    _L1_ffn_all = _L1_ffn_setup()
    _L1_ffn_in = {k: v for k, v in _L1_ffn_all.items() if k in ('weight', 'aux_weight1', 'aux_weight2', 'bias')}
    del _L1_ffn_all

    def _L2_xattn_setup():
        import jax, jax.numpy as jnp
        import numpy as np
        NUM_HEADS = 16
        key = jax.random.key(seed)
        ks = jax.random.split(key, 5)
        dim = 128
        B, N, N_c = (4, 128, 32)
        x = jax.random.normal(ks[0], (B, N, dim), dtype=jnp.float32)
        context = jax.random.normal(ks[1], (B, N_c, 2 * dim), dtype=jnp.float32)
        w_qkv = jax.random.normal(ks[2], (3 * dim, dim), dtype=jnp.float32) * 0.02
        w_proj = jax.random.normal(ks[3], (dim, dim), dtype=jnp.float32) * 0.02
        b_proj = jax.random.normal(ks[4], (dim,), dtype=jnp.float32) * 0.02
        return {'x': x, 'context': context, 'w_qkv': w_qkv, 'w_proj': w_proj, 'b_proj': b_proj}
    _L2_xattn_all = _L2_xattn_setup()
    _L2_xattn_in = {k: v for k, v in _L2_xattn_all.items() if k in ('w_qkv', 'w_proj', 'b_proj')}
    del _L2_xattn_all

    def _L2_ffn_setup():
        import jax, jax.numpy as jnp
        import numpy as np
        B, S, D, F, E, K = (4, 256, 128, 512, 8, 2)
        key = jax.random.key(seed)
        ks = jax.random.split(key, 8)
        x = jax.random.normal(ks[0], (B, S, D), dtype=jnp.float32)
        router_w = jax.random.normal(ks[1], (E, D), dtype=jnp.float32) * 0.02
        w1_w = jax.random.normal(ks[2], (E, F, D), dtype=jnp.float32) * 0.02
        w1_b = jax.random.normal(ks[3], (E, F), dtype=jnp.float32) * 0.02
        w2_w = jax.random.normal(ks[4], (E, D, F), dtype=jnp.float32) * 0.02
        w2_b = jax.random.normal(ks[5], (E, D), dtype=jnp.float32) * 0.02
        wg_w = jax.random.normal(ks[6], (E, F, D), dtype=jnp.float32) * 0.02
        wg_b = jax.random.normal(ks[7], (E, F), dtype=jnp.float32) * 0.02
        return {'x': x, 'router_w': router_w, 'w1_w': w1_w, 'w1_b': w1_b, 'w2_w': w2_w, 'w2_b': w2_b, 'wg_w': wg_w, 'wg_b': wg_b}
    _L2_ffn_all = _L2_ffn_setup()
    _L2_ffn_in = {k: v for k, v in _L2_ffn_all.items() if k in ('router_w', 'w1_w', 'w1_b', 'w2_w', 'w2_b', 'wg_w', 'wg_b')}
    del _L2_ffn_all

    def _L3_xattn_setup():
        import jax, jax.numpy as jnp
        import numpy as np
        B, S, T = (32, 64, 64)
        SRC_SIZE, TGT_SIZE, OUT_SIZE, NUM_HEAD = (256, 128, 128, 8)
        HEAD_DIM = OUT_SIZE // NUM_HEAD
        key = jax.random.key(seed)
        ks = jax.random.split(key, 12)
        src = jax.random.normal(ks[0], (B, S, SRC_SIZE), dtype=jnp.float32)
        tgt = jax.random.normal(ks[1], (B, T, TGT_SIZE), dtype=jnp.float32)
        src_mask = (jax.random.uniform(ks[2], (B, S)) > 0.3).astype(jnp.float32)
        src_mask = src_mask.at[:, 0].set(1.0)
        tgt_mask = (jax.random.uniform(ks[3], (B, T)) > 0.3).astype(jnp.float32)
        tgt_mask = tgt_mask.at[:, 0].set(1.0)

        def lin(k, out_f, in_f):
            return jax.random.normal(k, (out_f, in_f), dtype=jnp.float32) / np.sqrt(in_f)
        W_src = lin(ks[4], 2 * OUT_SIZE, SRC_SIZE)
        b_src = jnp.zeros((2 * OUT_SIZE,), jnp.float32)
        W_tgt = lin(ks[5], OUT_SIZE, TGT_SIZE)
        b_tgt = jnp.zeros((OUT_SIZE,), jnp.float32)
        W_out = lin(ks[6], OUT_SIZE, OUT_SIZE + TGT_SIZE)
        b_out = jnp.zeros((OUT_SIZE,), jnp.float32)
        return {'src': src, 'tgt': tgt, 'src_mask': src_mask, 'tgt_mask': tgt_mask, 'W_src': W_src, 'b_src': b_src, 'W_tgt': W_tgt, 'b_tgt': b_tgt, 'W_out': W_out, 'b_out': b_out}
    _L3_xattn_all = _L3_xattn_setup()
    _L3_xattn_in = {k: v for k, v in _L3_xattn_all.items() if k in ('W_src', 'b_src', 'W_tgt', 'b_tgt', 'W_out', 'b_out')}
    del _L3_xattn_all

    def _L3_ffn_setup():
        import jax, jax.numpy as jnp
        import numpy as np
        D = 128
        H = 256
        E = 8
        TOP_K = 2
        N_SHARED = 1
        B, S = (2, 128)
        key = jax.random.key(seed)
        ks = jax.random.split(key, 12)
        sc = 0.02
        return {'hidden': jax.random.normal(ks[0], (B, S, D), jnp.float32), 'router_w': jax.random.normal(ks[1], (D, E), jnp.float32) * sc, 'router_b': jnp.zeros((E,), jnp.float32), 'sw1': jax.random.normal(ks[2], (D, H), jnp.float32) * sc, 'sb1': jnp.zeros((H,), jnp.float32), 'sw2': jax.random.normal(ks[3], (H, D), jnp.float32) * sc, 'sb2': jnp.zeros((D,), jnp.float32), 'rw1': jax.random.normal(ks[4], (E, D, H), jnp.float32) * sc, 'rb1': jnp.zeros((E, H), jnp.float32), 'rw2': jax.random.normal(ks[5], (E, H, D), jnp.float32) * sc, 'rb2': jnp.zeros((E, D), jnp.float32)}
    _L3_ffn_all = _L3_ffn_setup()
    _L3_ffn_in = {k: v for k, v in _L3_ffn_all.items() if k in ('router_w', 'router_b', 'sw1', 'sb1', 'sw2', 'sb2', 'rw1', 'rb1', 'rw2', 'rb2')}
    del _L3_ffn_all
    return {'x': x, 'ctx_2048': ctx_2048, 'mask_BxS2_if0': mask_BxS2_if0, 'mask_BxS2_fk1': mask_BxS2_fk1, 'L0_xattn_Wq': _L0_xattn_in['Wq'], 'L0_xattn_Wkv': _L0_xattn_in['Wkv'], 'L0_xattn_null_kv': _L0_xattn_in['null_kv'], 'L0_xattn_Wout': _L0_xattn_in['Wout'], 'L0_xattn_ln_scale': _L0_xattn_in['ln_scale'], 'L0_xattn_ln_bias': _L0_xattn_in['ln_bias'], 'L0_ffn_W_r': _L0_ffn_in['W_r'], 'L0_ffn_W_k': _L0_ffn_in['W_k'], 'L0_ffn_W_v': _L0_ffn_in['W_v'], 'L0_ffn_mu_r': _L0_ffn_in['mu_r'], 'L0_ffn_mu_k': _L0_ffn_in['mu_k'], 'L1_xattn_W_in': _L1_xattn_in['W_in'], 'L1_xattn_b_in': _L1_xattn_in['b_in'], 'L1_xattn_g_res': _L1_xattn_in['g_res'], 'L1_xattn_g_init': _L1_xattn_in['g_init'], 'L1_ffn_weight': _L1_ffn_in['weight'], 'L1_ffn_aux_weight1': _L1_ffn_in['aux_weight1'], 'L1_ffn_aux_weight2': _L1_ffn_in['aux_weight2'], 'L1_ffn_bias': _L1_ffn_in['bias'], 'L2_xattn_w_qkv': _L2_xattn_in['w_qkv'], 'L2_xattn_w_proj': _L2_xattn_in['w_proj'], 'L2_xattn_b_proj': _L2_xattn_in['b_proj'], 'L2_ffn_router_w': _L2_ffn_in['router_w'], 'L2_ffn_w1_w': _L2_ffn_in['w1_w'], 'L2_ffn_w1_b': _L2_ffn_in['w1_b'], 'L2_ffn_w2_w': _L2_ffn_in['w2_w'], 'L2_ffn_w2_b': _L2_ffn_in['w2_b'], 'L2_ffn_wg_w': _L2_ffn_in['wg_w'], 'L2_ffn_wg_b': _L2_ffn_in['wg_b'], 'L3_xattn_W_src': _L3_xattn_in['W_src'], 'L3_xattn_b_src': _L3_xattn_in['b_src'], 'L3_xattn_W_tgt': _L3_xattn_in['W_tgt'], 'L3_xattn_b_tgt': _L3_xattn_in['b_tgt'], 'L3_xattn_W_out': _L3_xattn_in['W_out'], 'L3_xattn_b_out': _L3_xattn_in['b_out'], 'L3_ffn_router_w': _L3_ffn_in['router_w'], 'L3_ffn_router_b': _L3_ffn_in['router_b'], 'L3_ffn_sw1': _L3_ffn_in['sw1'], 'L3_ffn_sb1': _L3_ffn_in['sb1'], 'L3_ffn_sw2': _L3_ffn_in['sw2'], 'L3_ffn_sb2': _L3_ffn_in['sb2'], 'L3_ffn_rw1': _L3_ffn_in['rw1'], 'L3_ffn_rb1': _L3_ffn_in['rb1'], 'L3_ffn_rw2': _L3_ffn_in['rw2'], 'L3_ffn_rb2': _L3_ffn_in['rb2']}

def reference(x, ctx_2048, mask_BxS2_if0, mask_BxS2_fk1, L0_xattn_Wq, L0_xattn_Wkv, L0_xattn_null_kv, L0_xattn_Wout, L0_xattn_ln_scale, L0_xattn_ln_bias, L0_ffn_W_r, L0_ffn_W_k, L0_ffn_W_v, L0_ffn_mu_r, L0_ffn_mu_k, L1_xattn_W_in, L1_xattn_b_in, L1_xattn_g_res, L1_xattn_g_init, L1_ffn_weight, L1_ffn_aux_weight1, L1_ffn_aux_weight2, L1_ffn_bias, L2_xattn_w_qkv, L2_xattn_w_proj, L2_xattn_b_proj, L2_ffn_router_w, L2_ffn_w1_w, L2_ffn_w1_b, L2_ffn_w2_w, L2_ffn_w2_b, L2_ffn_wg_w, L2_ffn_wg_b, L3_xattn_W_src, L3_xattn_b_src, L3_xattn_W_tgt, L3_xattn_b_tgt, L3_xattn_W_out, L3_xattn_b_out, L3_ffn_router_w, L3_ffn_router_b, L3_ffn_sw1, L3_ffn_sb1, L3_ffn_sw2, L3_ffn_sb2, L3_ffn_rw1, L3_ffn_rb1, L3_ffn_rw2, L3_ffn_rb2):
    import jax
    import jax.numpy as jnp

    def _L0_xattn_ref(x, context, Wq, Wkv, null_kv, Wout, ln_scale, ln_bias):
        import jax, jax.numpy as jnp
        import numpy as np
        B, N, DIM = (8, 512, 128)
        M, CTX = (32, 256)
        HEADS, DH = (16, 64)
        INNER = HEADS * DH
        EPS = 1e-06

        def _split_heads(t):
            b, n, _ = t.shape
            return t.reshape(b, n, HEADS, DH).transpose(0, 2, 1, 3)
        scale = DH ** (-0.5)
        b = x.shape[0]
        q = _split_heads(jnp.einsum('bnd,df->bnf', x, Wq))
        kv = jnp.einsum('bmc,cf->bmf', context, Wkv)
        k, v = jnp.split(kv, 2, axis=-1)
        k, v = (_split_heads(k), _split_heads(v))
        nk = jnp.broadcast_to(null_kv[0], (b, HEADS, 1, DH))
        nv = jnp.broadcast_to(null_kv[1], (b, HEADS, 1, DH))
        k = jnp.concatenate((nk, k), axis=-2)
        v = jnp.concatenate((nv, v), axis=-2)
        q = q * scale
        sim = jnp.einsum('bhid,bhjd->bhij', q, k)
        attn = jax.nn.softmax(sim, axis=-1)
        out = jnp.einsum('bhij,bhjd->bhid', attn, v)
        out = out.transpose(0, 2, 1, 3).reshape(b, -1, INNER)
        out = jnp.einsum('bnf,fd->bnd', out, Wout)
        mu = jnp.mean(out, axis=-1, keepdims=True)
        var = jnp.var(out, axis=-1, keepdims=True)
        out = (out - mu) * jax.lax.rsqrt(var + EPS) * ln_scale + ln_bias
        return out

    def _L0_ffn_ref(x, W_r, W_k, W_v, mu_r, mu_k):
        import jax, jax.numpy as jnp
        import numpy as np
        DIM = 128

        def _reference_tuple_inner(x, W_r, W_k, W_v, mu_r, mu_k):
            B, T, C = x.shape
            x_prev = jnp.concatenate([jnp.zeros((B, 1, C), x.dtype), x[:, :-1, :]], axis=1)
            xr = mu_r * x + (1.0 - mu_r) * x_prev
            xk = mu_k * x + (1.0 - mu_k) * x_prev
            r = jax.nn.sigmoid(jnp.einsum('btc,dc->btd', xr, W_r))
            k = jnp.einsum('btc,dc->btd', xk, W_k)
            k_act = jnp.square(jax.nn.relu(k))
            out = r * jnp.einsum('btc,dc->btd', k_act, W_v)
            new_state = x[:, -1, :]
            return (out, new_state)
        return _reference_tuple_inner(x, W_r, W_k, W_v, mu_r, mu_k)[0]

    def _L1_xattn_ref(embeds, patch_embeds, patch_lens, W_in, b_in, g_res, g_init):
        import jax, jax.numpy as jnp
        import numpy as np
        B, L, P = (4, 512, 128)
        D_MODEL = 128
        D_GLOBAL = 256
        HEADDIM = 32
        EPSILON = 0.001
        RMS_EPS = 1e-05

        def rmsnorm(x, g, eps=RMS_EPS):
            var = jnp.mean(jnp.square(x), axis=-1, keepdims=True)
            return x * jax.lax.rsqrt(var + eps) * g

        def _hnet_depool(h, h_patch_full, patch_lens):
            h_patch = h_patch_full[..., :D_MODEL]
            bsz, plen = (h_patch.shape[0], h_patch.shape[1])
            seqlen = h.shape[1]
            logp = jnp.full((bsz, plen), -EPSILON, dtype=jnp.float32)
            bidx = jnp.cumsum(patch_lens, axis=1) - 1
            boundary_mask = jnp.zeros((bsz, seqlen), dtype=jnp.int32)
            boundary_mask = boundary_mask.at[jnp.arange(bsz)[:, None], bidx].set(1)
            dt = (-jnp.log(-jnp.expm1(logp))).astype(h_patch.dtype)
            x = h_patch / dt[..., None]
            n_heads = D_MODEL // HEADDIM
            A = -jnp.ones((n_heads,), dtype=jnp.float32)
            bcoef = jnp.exp(logp).astype(h_patch.dtype)
            x4 = x.reshape(bsz, plen, n_heads, HEADDIM)
            a = jnp.exp(dt[:, :, None] * A[None, None, :])
            u = (dt * bcoef)[:, :, None, None] * x4
            a_b = jnp.broadcast_to(a[..., None], u.shape)

            def comb(lft, rgt):
                aL, uL = lft
                aR, uR = rgt
                return (aL * aR, uL * aR + uR)
            _, s = jax.lax.associative_scan(comb, (a_b, u), axis=1)
            depool = s.reshape(bsz, plen, D_MODEL)
            plug = jnp.clip(jnp.cumsum(boundary_mask, axis=1) - 1, 0, plen - 1)
            depool_out = depool[jnp.arange(bsz)[:, None], plug]
            return depool_out + h
        h = rmsnorm(embeds, g_res)
        h = jnp.einsum('bld,ed->ble', h, W_in) + b_in
        h_patch = rmsnorm(patch_embeds, g_init)
        return _hnet_depool(h, h_patch, patch_lens)

    def _L1_ffn_ref(x, weight, aux_weight1, aux_weight2, bias):
        import jax, jax.numpy as jnp
        import numpy as np
        D_MODEL = 128
        h = jnp.einsum('btc,cd->btd', x, weight)
        h = jnp.einsum('btc,cd->btd', h, aux_weight1)
        h = jnp.einsum('btc,cd->btd', h, aux_weight2)
        return jnp.tanh(h + bias)

    def _L2_xattn_ref(x, context, w_qkv, w_proj, b_proj):
        import jax, jax.numpy as jnp
        import numpy as np
        NUM_HEADS = 16
        B, N, C = x.shape
        H = NUM_HEADS
        D = C // H
        scale = D ** (-0.5)
        qkv = (x @ w_qkv.T).reshape(B, N, 3, H, D).transpose(2, 0, 3, 1, 4)
        q, k, v = (qkv[0], qkv[1], qkv[2])
        N_c = context.shape[1]
        kv = context.reshape(B, N_c, 2, H, D).transpose(2, 0, 3, 1, 4)
        extra_k, extra_v = (kv[0], kv[1])
        k = jnp.concatenate([extra_k, k], axis=2)
        v = jnp.concatenate([extra_v, v], axis=2)
        dtype = q.dtype
        attn = jnp.einsum('bhnd,bhmd->bhnm', q * scale, k).astype(jnp.float32)
        attn = jax.nn.softmax(attn, axis=-1).astype(dtype)
        out = jnp.einsum('bhnm,bhmd->bhnd', attn, v)
        out = out.transpose(0, 2, 1, 3).reshape(B, N, C)
        return out @ w_proj.T + b_proj

    def _L2_ffn_ref(x, router_w, w1_w, w1_b, w2_w, w2_b, wg_w, wg_b):
        import jax, jax.numpy as jnp
        import numpy as np
        B, S, D, F, E, K = (4, 256, 128, 512, 8, 2)
        probs = jax.nn.softmax(jnp.einsum('bsd,ed->bse', x, router_w), axis=-1)
        token_probs, probs_idx = jax.lax.top_k(probs, K)
        gates = jnp.sum(token_probs[..., None] * jax.nn.one_hot(probs_idx, E, dtype=x.dtype), axis=-2)
        gates_e = jnp.moveaxis(gates, -1, 0)

        def body(acc, params):
            w1w, w1b, w2w, w2b, wgw, wgb, g = params
            y = jax.nn.gelu(jnp.einsum('bsd,fd->bsf', x, wgw) + wgb, approximate=False)
            h = y * (jnp.einsum('bsd,fd->bsf', x, w1w) + w1b)
            out = jnp.einsum('bsf,df->bsd', h, w2w) + w2b
            return (acc + out * g[..., None], None)
        acc0 = jnp.zeros_like(x)
        out, _ = jax.lax.scan(body, acc0, (w1_w, w1_b, w2_w, w2_b, wg_w, wg_b, gates_e))
        return out

    def _L3_xattn_ref(src, tgt, src_mask, tgt_mask, W_src, b_src, W_tgt, b_tgt, W_out, b_out):
        import jax, jax.numpy as jnp
        import numpy as np
        B, S, T = (32, 64, 64)
        SRC_SIZE, TGT_SIZE, OUT_SIZE, NUM_HEAD = (256, 128, 128, 8)
        HEAD_DIM = OUT_SIZE // NUM_HEAD
        b, s, _ = src.shape
        t = tgt.shape[1]
        src_trans = jnp.einsum('bsf,of->bso', src, W_src) + b_src
        tgt_trans = jnp.einsum('btf,of->bto', tgt, W_tgt) + b_tgt
        src_trans = src_trans * src_mask[:, :, None]
        tgt_trans = tgt_trans * tgt_mask[:, :, None]
        src_key, src_val = jnp.split(src_trans, 2, axis=2)
        k = src_key.reshape(b, s, NUM_HEAD, HEAD_DIM)
        v = src_val.reshape(b, s, NUM_HEAD, HEAD_DIM)
        q = tgt_trans.reshape(b, t, NUM_HEAD, HEAD_DIM)
        scores = jnp.einsum('bthd,bshd->bhts', q, k) / np.sqrt(HEAD_DIM)
        scores = jnp.where(src_mask[:, None, None, :] == 0, -jnp.inf, scores)
        attn = jax.nn.softmax(scores, axis=-1)
        tgt_update = jnp.einsum('bhts,bshd->bthd', attn, v).reshape(b, t, OUT_SIZE)
        cat_tgt = jnp.concatenate([tgt, tgt_update], axis=2)
        return jnp.einsum('btf,of->bto', cat_tgt, W_out) + b_out

    def _L3_ffn_ref(hidden, router_w, router_b, sw1, sb1, sw2, sb2, rw1, rb1, rw2, rb2):
        import jax, jax.numpy as jnp
        import numpy as np
        D = 128
        H = 256
        E = 8
        TOP_K = 2
        N_SHARED = 1
        B, S = (2, 128)
        b, s, d = hidden.shape
        T = b * s
        flat = hidden.reshape(T, d)
        router_logits = flat @ router_w + router_b
        router_probs = jax.nn.softmax(router_logits, axis=-1)
        topk_probs, topk_idx = jax.lax.top_k(router_probs, TOP_K)
        weights = jnp.zeros_like(router_probs).at[jnp.arange(T)[:, None], topk_idx].add(topk_probs)
        sh = jax.nn.gelu(flat @ sw1 + sb1, approximate=False)
        shared_out = (sh @ sw2 + sb2) / N_SHARED
        h1 = jax.nn.gelu(jnp.einsum('td,edh->teh', flat, rw1) + rb1[None], approximate=False)
        expert_out = jnp.einsum('teh,ehd->ted', h1, rw2) + rb2[None]
        mixed = jnp.einsum('ted,te->td', expert_out, weights)
        return (shared_out + mixed).reshape(b, s, d)
    x = x + _L0_xattn_ref(_layernorm(x, axis=-1), ctx_2048, L0_xattn_Wq, L0_xattn_Wkv, L0_xattn_null_kv, L0_xattn_Wout, L0_xattn_ln_scale, L0_xattn_ln_bias)
    x = x + _L0_ffn_ref(_layernorm(x, axis=-1), L0_ffn_W_r, L0_ffn_W_k, L0_ffn_W_v, L0_ffn_mu_r, L0_ffn_mu_k)
    x = x + _L1_xattn_ref(_layernorm(x, axis=-1), ctx_2048, mask_BxS2_if0, L1_xattn_W_in, L1_xattn_b_in, L1_xattn_g_res, L1_xattn_g_init)
    x = x + _L1_ffn_ref(_layernorm(x, axis=-1), L1_ffn_weight, L1_ffn_aux_weight1, L1_ffn_aux_weight2, L1_ffn_bias)
    x = x + _L2_xattn_ref(_layernorm(x, axis=-1), ctx_2048, L2_xattn_w_qkv, L2_xattn_w_proj, L2_xattn_b_proj)
    x = x + _L2_ffn_ref(_layernorm(x, axis=-1), L2_ffn_router_w, L2_ffn_w1_w, L2_ffn_w1_b, L2_ffn_w2_w, L2_ffn_w2_b, L2_ffn_wg_w, L2_ffn_wg_b)
    x = x + _L3_xattn_ref(ctx_2048, _layernorm(x, axis=-1), mask_BxS2_fk1, mask_BxS2_fk1, L3_xattn_W_src, L3_xattn_b_src, L3_xattn_W_tgt, L3_xattn_b_tgt, L3_xattn_W_out, L3_xattn_b_out)
    x = x + _L3_ffn_ref(_layernorm(x, axis=-1), L3_ffn_router_w, L3_ffn_router_b, L3_ffn_sw1, L3_ffn_sb1, L3_ffn_sw2, L3_ffn_sb2, L3_ffn_rw1, L3_ffn_rb1, L3_ffn_rw2, L3_ffn_rb2)
    return x

_drawn_inputs = setup_inputs


def setup_inputs(seed=0):
    import zlib

    import numpy as np

    out = dict(_drawn_inputs(seed))
    spreads = {'L0_xattn_ln_scale': (1.0, 0.2),
     'L0_xattn_ln_bias': (0.0, 0.1),
     'L1_xattn_b_in': (0.0, 0.1),
     'L1_xattn_g_res': (1.0, 0.6),
     'L1_xattn_g_init': (1.0, 0.2),
     'L1_ffn_bias': (0.0, 0.1),
     'L3_xattn_b_src': (0.0, 0.331),
     'L3_xattn_b_tgt': (0.0, 2.0),
     'L3_xattn_b_out': (0.0, 0.329),
     'L3_ffn_router_b': (0.0, 0.8),
     'L3_ffn_sb1': (0.0, 2.0),
     'L3_ffn_sb2': (0.0, 0.511),
     'L3_ffn_rb1': (0.0, 0.8),
     'L3_ffn_rb2': (0.0, 0.715)}
    factors = {'L0_xattn_null_kv': 8.0,
     'L0_ffn_W_r': 4.482,
     'L0_ffn_mu_r': 8.0,
     'L1_ffn_weight': 8.0,
     'L1_ffn_aux_weight1': 8.0,
     'L1_ffn_aux_weight2': 8.0,
     'L2_xattn_w_qkv': 5.873,
     'L2_xattn_b_proj': 5.492,
     'L2_ffn_router_w': 8.0,
     'L2_ffn_w1_w': 8.0,
     'L2_ffn_w1_b': 8.0,
     'L2_ffn_w2_w': 8.0,
     'L2_ffn_w2_b': 8.0,
     'L2_ffn_wg_w': 8.0,
     'L2_ffn_wg_b': 8.0,
     'L3_ffn_router_w': 5.219,
     'L3_ffn_sw1': 3.052,
     'L3_ffn_rw1': 8.0,
     'L3_ffn_rw2': 8.0}
    for name, (base, spread) in spreads.items():
        noise = np.random.default_rng([zlib.crc32(name.encode()), seed]).standard_normal(out[name].shape)
        drawn = base * np.exp(spread * noise) if base else spread * noise
        out[name] = jnp.asarray(drawn.astype(out[name].dtype))
    for name, factor in factors.items():
        out[name] = (out[name] * factor).astype(out[name].dtype)
    return out
```

```python
from contextlib import ExitStack

import numpy as np

import concourse.bass as bass
from concourse import mybir

F32 = mybir.dt.float32
F32R = mybir.dt.float32r
BF16 = mybir.dt.bfloat16
I32 = mybir.dt.int32
ALU = mybir.AluOpType
ACT = mybir.ActivationFunctionType
AX = mybir.AxisListType

P = 128
B, T, D = 8, 256, 128
CTX = 256
PAIRS = B // 2
TT = T // P
NT = 2 * TT
N = 2 * T
EPS = 1e-5
EPS_OUT = 1e-6
GH = 4
RING = 3

H0, D0 = 16, 64
H2, D2 = 16, 8
H3, D3 = 8, 16
NE = 8
F2 = 512
FT2 = F2 // P
F3 = 256
FT3 = F3 // P
E3 = NE + 1
NEG = -1.0e30

SLOT2, SLOT3 = 32, 64
MASKROW = 48
MROW = P - 1


class Attn:

    def __init__(self, name, groups_of_batch, halves, scale, srow):
        self.name, self.gpb, self.halves, self.scale, self.srow = name, groups_of_batch, halves, scale, srow
        self.groups = 2 * groups_of_batch
        self.phases = 4 if name == "L0" else 3
        self.items = GH * halves
        self.keys = 2 * P * halves


A0 = Attn("L0", H0 // GH, 1, float(D0) ** -0.5, D0)
A2 = Attn("L2", H2 // GH, 2, float(D2) ** -0.5, MROW)
A3 = Attn("L3", H3 // GH, 1, float(D3) ** -0.5, MROW)


def order(a):
    yield "project", 0, 0
    yield "take", 0, 0
    if a is A2:
        yield "before", 0, 0
        yield "split", 0, 0
    yield "project", 0, 1
    yield "take", 0, 1
    if a is not A2:
        yield "split", 0, 0
    yield "split", 0, 1
    if a is not A2:
        yield "before", 0, 0
    for step, g, n in START:
        yield step, g, n
    late = []
    for u in range(a.groups):
        near, far = u + 1 < a.groups, u + 2 < a.groups
        for step in STEPS_OF[a.name].split():
            kind, n = step[:-1], int(step[-1])
            if kind == "exp":
                yield "exp", u, n
                if n % GH == GH - 1:
                    late.append(("values", u, n // GH))
                    if n == a.items - 1 and u % a.gpb == a.gpb - 1:
                        late += [("tail", u // a.gpb, phase) for phase in range(a.phases)]
            elif kind == "values":
                if late and late[0][0] == "values":
                    yield late.pop(0)
            elif kind == "tail":
                if late and late[0][0] == "tail":
                    yield late.pop(0)
            elif kind in ("scores", "turn"):
                if near:
                    yield kind, u + 1, n
            elif far:
                yield kind, u + 2, n
    yield from late


START = (("scores", 0, 0), ("scores", 0, 1), ("project", 1, 0), ("take", 1, 0), ("scores", 0, 2), ("split", 1, 0),
         ("scores", 0, 3), ("project", 1, 1), ("turn", 0, 0), ("take", 1, 1), ("split", 1, 1))
STEPS_OF = {
    "L0": "scores0 exp0 scores1 tail0 exp1 scores2 project0 scores3 take0 tail0 exp2 project1 tail0 turn0 take1 values0 "
          "tail0 exp3",
    "L2": "scores0 exp0 scores1 project0 take0 exp1 values0 tail0 split0 exp2 tail0 scores2 exp3 tail0 scores3 project1 "
          "turn0 take1 exp4 exp5 values0 exp6 split1 exp7",
    "L3": "scores0 exp0 scores1 project0 take0 scores2 exp1 scores3 tail0 split0 project1 turn0 take1 exp2 tail0 "
          "values0 tail0 exp3 split1",
}

EARLY = [("wq0", H0 * D0), ("ident", P), ("wk0", 2 * H0 * D0), ("wv0", 2 * H0 * D0),
         ("tri", 2 * T), ("decay", 2 * T), ("iota", T), ("srow", 2), ("nkcol", 1), ("esum", 4 * 32),
         ("nullv", H0 // 2 * P), ("wout0", H0 // 2 * D), ("sel0", H0 // 2 * P), ("wcT", D),
         ("a1", D), ("a2", D)]
LATE = [("wr", D), ("wk", D), ("wv", D), ("mu", 2), ("win", D), ("gres", 1),
        ("wq2", 4 * P), ("wk2", 4 * P), ("perm2", 4 * P), ("wv2", D), ("wp2", 2 * D), ("rt2", NE),
        ("bg2", NE * FT2), ("b12", NE * FT2), ("gb", 9), ("b2e", D), ("etri", NE * NE),
        ("wq3", 4 * P), ("wk3", 2 * 4 * P), ("bq3", 4), ("bk3", 4), ("msel", 4), ("wv3", 2 * D),
        ("wox3", D), ("wo3", 2 * D), ("rt3", NE), ("fw1", E3 * F3), ("fb1", E3 * FT3),
        ("fw2", E3 * FT3 * D), ("fb2", D)]
ROWS = [("nk", D0), ("ls0", D), ("lb0", D), ("ginit", D), ("bin", D), ("bff1", D), ("bp2", D),
        ("bv3", D), ("bo3", D), ("rb3", NE), ("sb2", D)]
SCRATCH = ("tri", "nullv", "wcT", "a1", "a2")


def signals():
    s = {}
    s.update(w_early=0, w_late=0, rows=0, pl=0, pre_dve=0, pre_pe=0, pre_act=0, pre_pool=0)
    s.update(x_in=16, ctx_in=64)
    s.update(stored=16, x_out=1)
    s.update(dve=0, pool=0)
    s.update(mv=8, rs=8, xn=8 * NT, tr=8, xT=8)
    s.update(p_ss=1, p_rp=1, p_hp=1, p_eq=1, p_bd=1, p_bds=1, p_pb=1, p_g=1, p_dep=1, p_deps=1,
             p_pd=1, p_pds=1)
    for a in (A0, A2, A3):
        g, n = a.groups, a.name
        s.update({f"{n}proj": 2 * g, f"{n}score": 8 * g, f"{n}max": 8 * g, f"{n}mt": g, f"{n}mte": g,
                  f"{n}mrow": 16 * g, f"{n}st": a.items * g, f"{n}p": a.items * g,
                  f"{n}pv": a.halves * g})
    s.update(L0act=2 * 2 * A0.groups, L0qkr=2 * A0.groups, L0v=8, L0ve=8, L0o=A0.groups, L0oe=A0.groups,
             L0nul=2, L0pn=2, L0rr=2, L0r=8, L0rm=8, L0y=2, L0ys=2, L0yr=2, L0yx=2, L0init=1, xlb=1)
    s.update(f_0=1, f_a=1, f_r=1, f_k=1, f_rp=1, f_kp=1, f_th=1, f_ka=1, f_v=1)
    s.update(L1w=1, L1y=1, L1fy=1, L1fb=1, L1ft=1)
    s.update(L2bp=2 * A2.groups, L2k=A2.groups, L2q=GH * A2.groups, L2v=1, L2ve=4, L2ext=1,
             L2init=1, L2xb=1)
    s.update(L3tm=2 * A3.groups, L3bp=2 * A3.groups,
             L3k=2 * A3.groups, L3q=GH * A3.groups, L3v=1, L3vt=1, L3ve=1, L3mask=1, L3init=1, L3xb=1)
    for n in ("L2", "L3"):
        s.update({f"{n}oe": 2, f"{n}tn": 2, f"{n}on": 2, f"{n}tb": 2, f"{n}ont": 2, f"{n}y": 2,
                  f"{n}yx": 2})
        s.update({f"{n}lg": 1, f"{n}dl": 1, f"{n}ex": 1, f"{n}gate": 1, f"{n}gt": 1, f"{n}gts": 1,
                  f"{n}bias": 1, f"{n}acc0": 1})
    ne2, ne3 = NE * FT2, E3 * FT3
    s.update(g_zg=ne2, g_z1=ne2, g_gl=ne2, g_h=ne2, g_y=ne2, g_ty=NE, g_acc=NE)
    s.update(h_z=ne3, h_h=ne3, h_y=ne3, h_ty=E3, h_acc=E3)
    s.update(w_in0=64, w_in1=64, sb2x=1)
    return s


def program(nc, t, steps):
    sig = signals()
    sig.update(dve=steps[0], pool=steps[1])
    made = {}
    with ExitStack() as ctx:
        def sb(name, shape, dt=F32, where=None):
            return (where or ctx).enter_context(nc.sbuf_tensor(name + "_sb", shape, dt))

        S = {n: ctx.enter_context(nc.semaphore(n + "_sem")) for n in sig}

        w = {n: sb(n, [P, c]) for n, c in EARLY + LATE if n not in SCRATCH}
        r = {n: sb(n, [P, c]) for n, c in ROWS}
        xin = sb("xin", [P, NT, D])
        x = sb("x", [P, NT, D])
        xb = sb("xb", [P, NT, D])
        xn = sb("xn", [P, NT, D])
        xnT = sb("xnT", [P, N])
        ctxT = sb("ctxT", [P, 2, 2, T])
        ctxN = sb("ctxN", [P, NT, CTX])
        maskB = sb("maskB", [P, N])
        maskC = sb("maskC", [P, NT])
        pdb = sb("pdb", [P, NT, D])
        st6 = sb("st6", [P, NT, 6])
        mv = sb("mv", [P, NT, 2])
        rs = sb("rs", [P, NT])
        rt = sb("rt", [P, NT])
        half = sb("half", [P, NT])
        ss = sb("ss", [P, NT])
        cum = sb("cum", [P, 2, PAIRS, 2 * TT])
        cc = sb("cc", [P, 2, 2 * TT])
        trib = sb("trib", [P, 2, T], BF16)
        oneb = sb("oneb", [P, P], BF16)
        wn0 = sb("wn0", [P, P])
        nvw = sb("nvw", [P, D])
        wc = sb("wc", [P, D])
        nm = sb("nm", [P, 2, TT, GH])
        nmS = sb("nmS", [P, 2, TT, P])
        mT = sb("mT", [GH, T])
        mTr = sb("mTr", [GH, T], F32R)
        pbuf = sb("pbuf", [P, 2, GH, 2 * T])
        tmp = sb("tmp", [P, N])
        tmp2 = sb("tmp2", [P, N])
        stream = sb("stream", [P, 2, 3, F2])
        gl = sb("gl", [P, 2, N])
        hb = sb("hb", [P, 3, N])
        lg = sb("lg", [P, NT, NE])
        ex = sb("ex", [P, NT, NE])
        pr = sb("pr", [P, NT, NE])
        r4 = sb("r4", [P, 2, NT])
        rank = tmp[:, 0:NT * NE * NE].rearrange("p (n e k) -> p n e k", n=NT, e=NE)
        rank2 = tmp2[:, 0:NT * NE * NE].rearrange("p (n e k) -> p n e k", n=NT, e=NE)
        gates = sb("gates", [P, NT, NE])
        gT = tmp2[0:NE, :]

        on = sb("on", [P, NT, P])
        om = sb("om", [P, 2])
        pn = sb("pn", [P, T])
        rr = sb("rr", [P, T])
        win = pn[:, 0:D]

        def region():
            return ExitStack()

        with region() as part:
            qk0 = sb("qk0", [P, RING, GH, 2, T + 2], F32, part)
            qkr0 = sb("qkr0", [P, 2, 2, 2, T + 2], F32R, part)
            v0 = sb("v0", [P, 2, TT, H0 * D0], F32, part)
            with region() as early:
                eqb = sb("eqb", [P, 2, TT, T], BF16, early)
                bds = sb("bds", [P, NT, P], BF16, early)
            oT0 = sb("oT0", [P, H0 // 2, T], F32, part)
        with region() as part:
            q2 = sb("q2", [P, RING, GH, T], F32R, part)
            k2 = sb("k2", [P, RING, 2 * T], F32R, part)
            v2 = sb("v2", [P, 2, 4, H2, 32], F32, part)
            q3 = sb("q3", [P, RING, GH, T], F32R, part)
            k3 = sb("k3", [P, RING, 2, T], F32R, part)
            v3 = sb("v3", [P, 2, TT, H3, 32], F32, part)
        with region() as part:
            scratch = {n: sb(n, [P, c], F32, part) for n, c in EARLY if n in SCRATCH}
            pli = sb("pli", [P, 2, B], I32, part)
            plf = sb("plf", [P, 2, B], F32, part)
            wcomb = sb("wcomb", [P, D], F32, part)
            wnt = sb("wnt", [P, H0, D0], F32, part)
            wnr = sb("wnr", [P, H0], F32, part)
        w.update(scratch)
        hps = gl[:, 0, :].rearrange("p (n d) -> p n d", n=NT)
        gsel = hb[:, 0:2, :].rearrange("p s (b t) -> p s b t", b=2)
        dep = gl[:, 1, :].rearrange("p (n d) -> p n d", n=NT)
        bpart = [hb[:, 2, :].bitcast(F32R), gl[:, 1, :].bitcast(F32R)]
        oe = hb[:, 0, :]
        ont = hb[:, 1, :].rearrange("p (n d) -> p n d", n=NT)
        mqk = v2[:, 0, :, :, :].rearrange("p j h w -> p (j h w)")[:, 0:4 * T].rearrange("p (b k t) -> p b k t", b=2, k=2)
        xr, xk = gl[:, 0, :], gl[:, 1, :]
        ka = hb[:, 2, :]

        bank = [ctx.enter_context(nc.psum_tensor(f"bank{i}", [P, 512], F32)) for i in range(8)]
        SB_, TB, OB, PJ, PX = bank[0:2], bank[2:4], bank[4:6], bank[6], bank[7]

        def turn(eng, it):
            base = {}
            for k in sorted({sig[n] for n in sig if sig[n]}):
                base[k] = eng.alloc_register(f"base{k}")
                eng.reg_alu(base[k], it, k, ALU.mult)
            return base, eng.alloc_register("count")

        def count(eng, regs, name, n=None, cut=False):
            base, value = regs
            n = sig[name] if n is None else n
            assert 0 < n <= sig[name], (name, n)
            eng.reg_add(value, base[sig[name]], n)
            if cut:
                eng.wait_ge(S[name], 1)
            return value

        def four(ap):
            return ap.rearrange("p (n d) -> p n d", n=NT)

        block = ctx.enter_context(nc.Block())

        def stack_row(a, u):
            if a is A0:
                return qk0[D0:D0 + 1, u % RING, :, 0, 0:T], mT[:, :]
            q = q2 if a is A2 else q3
            return q[MROW:MROW + 1, u % RING, :, :].bitcast(F32), mTr[:, :].bitcast(F32)

        @block.sync
        def _(sp):
            def load_pair(i):
                sp.dma_start(xin[:, :, :], t["x"][i].rearrange("p (n d) -> p n d", n=NT)).then_inc(S["x_in"], 16)
                sp.dma_start(ctxT[:, :, :, :], t["ctxT"][i].rearrange("p (k b j) -> p k b j", k=2, b=2)).then_inc(S["ctx_in"], 16)
                sp.dma_start(ctxN[:, :, :], t["ctxN"][i].rearrange("p (n d) -> p n d", n=NT)).then_inc(S["ctx_in"], 16)
                sp.dma_start(maskB[:, :], t["maskrow"][i].broadcast_to([P, N])).then_inc(S["ctx_in"], 16)
                sp.dma_start(maskC[:, :], t["maskcol"][i]).then_inc(S["ctx_in"], 16)

            load_pair(0)
            for n, c in EARLY:
                sp.dma_start(w[n][:, :], t[n]).then_inc(S["w_early"], 16)
            for n, c in ROWS:
                sp.dma_start(r[n][:, :], t["row_" + n].broadcast_to([P, c])).then_inc(S["rows"], 16)
            sp.dma_start(pli[:, :, :], t["pl"].rearrange("p (a b) -> p a b", a=2)).then_inc(S["pl"], 16)
            for n, c in LATE:
                sp.dma_start(w[n][:, :], t[n]).then_inc(S["w_late"], 16)

            with sp.Fori(0, PAIRS) as it:
                regs = turn(sp, it)

                def at_cut(name, n=None):
                    return count(sp, regs, name, n, cut=True)

                def rows_of_maxima(a):
                    for u in range(a.groups):
                        sp.wait_ge(S[a.name + "mte"], at_cut(a.name + "mte", u + 1))
                        dst, src = stack_row(a, u)
                        sp.dma_start(dst, src).then_inc(S[a.name + "mrow"], 16)

                def expert(e):
                    if e >= 2:
                        sp.wait_ge(S["g_y"], at_cut("g_y", FT2 * (e - 1)))
                    sp.dma_start(stream[:, e % 2, :, :], t["experts"][e].rearrange("p (k f) -> p k f", k=3))\
                      .then_inc(S[f"w_in{e % 2}"], 16)

                rows_of_maxima(A0)
                expert(0)
                expert(1)
                rows_of_maxima(A2)
                for e in range(2, NE):
                    expert(e)
                rows_of_maxima(A3)
                sp.wait_ge(S["xn"], at_cut("xn", NT))
                for name in ("xlb", "p_ss", "p_hp", "L2ext", "L3proj", "L3v", "L3ve", "L3mask"):
                    sp.wait_ge(S[name], at_cut(name))
                load_pair((it + 1) % PAIRS)
                sp.wait_ge(S["x_out"], at_cut("x_out"))
                sp.dma_start(t["out"][it].rearrange("p (n d) -> p n d", n=NT), xb[:, :, :]).then_inc(S["stored"], 16)
            sp.wait_ge(S["stored"], 16 * (PAIRS + 1))
            sp.wait_ge(S["x_in"], 16 * (PAIRS + 1))
            sp.wait_ge(S["ctx_in"], 64 * (PAIRS + 1))

        @block.tensor
        def _(pe):
            mm = nc.tensor.matmul
            ident = w["ident"]

            pe.wait_ge(S["w_early"], 16 * len(EARLY))
            pe.wait_ge(S["pre_dve"], 1)
            for p in range(2):
                for q in range(2):
                    m = mm(bank[0][:, p * B:(p + 1) * B], w["tri"][:, q * T + p * P:q * T + (p + 1) * P],
                           plf[:, q, :], start=(p == 0 and q == 0), stop=(q == 1), skip_group_check=True)
            m.then_inc(S["pre_pe"], 1)
            for q in range(H0 // 2):
                m = mm(bank[1][:, 0:D], w["nullv"][:, q * P:(q + 1) * P], w["wout0"][:, q * D:(q + 1) * D],
                       start=(q == 0), stop=(q == H0 // 2 - 1))
            m.then_inc(S["pre_pe"], 1)
            mm(bank[2][:, 0:D], w["a1"][:, :], w["wcT"][:, :], start=True, stop=True).then_inc(S["pre_pe"], 1)
            pe.wait_ge(S["pre_act"], 1)
            mm(bank[3][:, 0:D], wcomb[:, :], w["a2"][:, :], start=True, stop=True).then_inc(S["pre_pe"], 1)

            pe.wait_ge(S["pre_dve"], 9)

            with pe.Fori(0, PAIRS) as it:
                regs = turn(pe, it)

                def at(name, n=None):
                    return count(pe, regs, name, n)

                def norm_transposes(part):
                    for n in range(NT):
                        pe.wait_ge(S["xn"], at("xn", NT * part + n + 1))
                        m = pe.transpose(PX[:, n * P:(n + 1) * P], xn[:, n, :], ident[:, :])
                    m.then_inc(S["tr"], 1)

                def depool_1():
                    pe.wait_ge(S["p_eq"], at("p_eq"))
                    for b in range(2):
                        for q in range(TT):
                            for p in range(2):
                                m = mm(SB_[0][:, (b * TT + q) * P:(b * TT + q + 1) * P],
                                       eqb[:, b, p, q * P:(q + 1) * P], oneb[:, :],
                                       start=(b == q == p == 0), stop=(p == 1), skip_group_check=True)
                    m.then_inc(S["p_bd"], 1)
                    pe.wait_ge(S["p_hp"], at("p_hp"))
                    for b in range(2):
                        for s in range(TT):
                            for q in range(s + 1):
                                m = mm(OB[0][:, (b * TT + s) * P:(b * TT + s + 1) * P],
                                       w["decay"][:, q * T + s * P:q * T + (s + 1) * P], hps[:, b * TT + q, :],
                                       start=(b == s == q == 0), stop=(q == s), skip_group_check=True)
                    m.then_inc(S["p_dep"], 1)

                def depool_2():
                    pe.wait_ge(S["p_bds"], at("p_bds"))
                    for b in range(2):
                        for q in range(TT):
                            m = mm(SB_[1][:, b * T:(b + 1) * T], bds[:, b * TT + q, :], trib[:, q, :],
                                   start=(b == q == 0), stop=(q == 1), skip_group_check=True)
                    m.then_inc(S["p_pb"], 1)

                def depool_3():
                    pe.wait_ge(S["p_g"], at("p_g"))
                    pe.wait_ge(S["p_deps"], at("p_deps"))
                    for b in range(2):
                        for q in range(TT):
                            for s in range(TT):
                                m = mm(OB[1][:, (b * TT + q) * P:(b * TT + q + 1) * P],
                                       gsel[:, s, b, q * P:(q + 1) * P], dep[:, b * TT + s, :],
                                       start=(b == q == s == 0), stop=(s == 1), skip_group_check=True)
                    m.then_inc(S["p_pd"], 1)

                def project0(u, q):
                    b, pair = u // A0.gpb, 2 * (u % A0.gpb) + q
                    cols = slice(pair * P, (pair + 1) * P)
                    n = 2 * u + q
                    if n:
                        pe.wait_ge(S["L0act"], at("L0act", 2 * n))
                        pe.wait_ge(S["L0qkr"], at("L0qkr", n))
                    mm(PJ[:, 0:T], w["wq0"][:, cols], xnT[:, b * T:(b + 1) * T], start=True, stop=True)
                    for k in range(2):
                        m = mm(PJ[:, T:2 * T], w["wk0"][:, k * H0 * D0:][:, cols], ctxT[:, k, b, :],
                               start=(k == 0), stop=(k == 1), skip_group_check=True)
                    m.then_inc(S["L0proj"], 1)

                def project2(u, q):
                    b, s = u // A2.gpb, u % A2.gpb
                    if 2 * u + q:
                        pe.wait_ge(S["L2k"], at("L2k", u)) if q == 0 else pe.wait_ge(S["L2q"], at("L2q", GH * (u + 1)))
                    sl = slice(s * P, (s + 1) * P)
                    if q == 0:
                        m = mm(PJ[:, 0:T], w["wq2"][:, sl], xnT[:, b * T:(b + 1) * T], start=True, stop=True)
                    else:
                        mm(PJ[:, 0:T], w["perm2"][:, sl], ctxT[:, 0, b, :], start=True, stop=True)
                        m = mm(PJ[:, T:2 * T], w["wk2"][:, sl], xnT[:, b * T:(b + 1) * T],
                               start=True, stop=True, skip_group_check=True)
                    m.then_inc(S["L2proj"], 1)

                def project3(u, q):
                    b, s = u // A3.gpb, 2 * (u % A3.gpb) + q
                    n = 2 * u + q
                    if n:
                        pe.wait_ge(S["L3tm"], at("L3tm", n))
                    mm(PJ[:, 0:T], w["wq3"][:, s * P:(s + 1) * P], xnT[:, b * T:(b + 1) * T], start=True, stop=True)
                    for k in range(2):
                        m = mm(PJ[:, T:2 * T], w["wk3"][:, (k * 4 + s) * P:(k * 4 + s + 1) * P], ctxT[:, k, b, :],
                               start=(k == 0), stop=(k == 1), skip_group_check=True)
                    m.then_inc(S["L3proj"], 1)

                def scores(a, u, c):
                    for i in range(TT):
                        n = 8 * u + TT * c + i
                        if n >= 2:
                            pe.wait_ge(S[a.name + "max"], at(a.name + "max", n - 1))
                        dst = SB_[n % 2]
                        if a is A0:
                            if i == 0 and c % 2 == 0:
                                pe.wait_ge(S["L0qkr"], at("L0qkr", 2 * u + c // 2 + 1))
                            rows = slice(D0 * (c % 2), D0 * (c % 2 + 1))
                            m = mm(dst[:, 0:T + 2], qkr0[rows, u % 2, c // 2, 0, i * P:(i + 1) * P],
                                   qkr0[rows, u % 2, c // 2, 1, :],
                                   start=True, stop=True)
                        elif a is A2:
                            if i == 0 and c == 0:
                                pe.wait_ge(S["L2q"], at("L2q", GH * (u + 1)))
                                pe.wait_ge(S["L2k"], at("L2k", u + 1))
                            m = mm(dst[:, :], q2[0:MROW, u % RING, c, i * P:(i + 1) * P], k2[0:MROW, u % RING, :],
                                   start=True, stop=True)
                        else:
                            if i == 0 and c % 2 == 0:
                                pe.wait_ge(S["L3q"], at("L3q", 2 * (2 * u + c // 2 + 1)))
                                pe.wait_ge(S["L3k"], at("L3k", 2 * u + c // 2 + 1))
                            m = mm(dst[:, 0:T], q3[0:MROW, u % RING, c, i * P:(i + 1) * P],
                                   k3[0:MROW, u % RING, c // 2, :], start=True, stop=True)
                        m.then_inc(S[a.name + "score"], 1)

                def turn_maxima(a, u):
                    pe.wait_ge(S[a.name + "max"], at(a.name + "max", 8 * (u + 1)))
                    if u:
                        pe.wait_ge(S[a.name + "mte"], at(a.name + "mte", u))
                    if a is A0 and u == a.gpb + 2:
                        pe.wait_ge(S["L0yx"], at("L0yx", 1))
                    for i in range(TT):
                        src = nmS[:, u // a.gpb, i, u % a.gpb:P:32] if a is A0 else nm[:, u % 2, i, :]
                        m = pe.transpose(PX[0:GH, i * P:(i + 1) * P], src, ident[:, :])
                    m.then_inc(S[a.name + "mt"], 1)

                def scores_T(a, u, h, c):
                    n = a.items * u + GH * h + c
                    if n >= 2:
                        pe.wait_ge(S[a.name + "p"], at(a.name + "p", n - 1))
                    if h == c == 0:
                        pe.wait_ge(S[a.name + "mrow"], at(a.name + "mrow", 16 * (u + 1)))
                    dst = TB[n % 2]
                    for j in range(2):
                        key = slice((2 * h + j) * P, (2 * h + j + 1) * P)
                        if a is A0:
                            k, q = qk0[0:D0 + 1, u % RING, c, 1, key], qk0[0:D0 + 1, u % RING, c, 0, 0:T]
                        elif a is A2:
                            k, q = k2[:, u % RING, key], q2[:, u % RING, c, :]
                        else:
                            k, q = k3[:, u % RING, c // 2, key], q3[:, u % RING, c, :]
                        m = mm(dst[:, j * T:(j + 1) * T], k, q, start=(j == 0), stop=(j == 1), skip_group_check=True)
                    m.then_inc(S[a.name + "st"], 1)

                def values(a, u, h):
                    pe.wait_ge(S[a.name + "p"], at(a.name + "p", a.items * u + GH * (h + 1)))
                    b, g = u // a.gpb, u % a.gpb
                    buf = (a.halves * u + h) % 2
                    if a is A0:
                        if u:
                            pe.wait_ge(S["L0oe"], at("L0oe", u))
                        for q in range(2):
                            for j in range(2):
                                for c in range(2):
                                    head = GH * g + 2 * q + c
                                    m = mm(OB[0][64 * c:64 * c + 64, q * T:(q + 1) * T],
                                           v0[:, b, j, head * D0:(head + 1) * D0],
                                           pbuf[:, buf, 2 * q + c, j * T:(j + 1) * T],
                                           start=(j == 0), stop=(j == 1), skip_group_check=True)
                        m.then_inc(S["L0o"], 1)
                        if b and g == 0:
                            pe.wait_ge(S["L0rm"], at("L0rm", 4))
                        for j in range(2):
                            for c in range(GH):
                                m = mm(OB[1][32 * c:32 * c + 32, 0:T], w["esum"][:, g * 32:(g + 1) * 32],
                                       pbuf[:, buf, c, j * T:(j + 1) * T],
                                       start=(g == j == 0), stop=(g == a.gpb - 1 and j == 1), skip_group_check=True)
                        m.then_inc(S["L0pv"], 1)
                        return
                    if b and g == h == 0:
                        pe.wait_ge(S[a.name + "oe"], at(a.name + "oe", 1))
                    vv = v2 if a is A2 else v3
                    of_set = H2 // (2 * GH) if a is A2 else 1
                    s, first = g // of_set, g % of_set == 0
                    for j in range(2):
                        for c in range(GH):
                            m = mm(OB[0][32 * c:32 * c + 32, s * T:(s + 1) * T], vv[:, b, 2 * h + j, GH * g + c, :],
                                   pbuf[:, buf, c, j * T:(j + 1) * T], start=(first and h == j == 0),
                                   stop=(g % of_set == of_set - 1 and h == a.halves - 1 and j == 1),
                                   skip_group_check=True)
                    m.then_inc(S[a.name + "pv"], 1)

                def finish0(b, phase):
                    if phase == 0:
                        pe.wait_ge(S["L0mte"], at("L0mte", A0.gpb * (b + 1) if b else A0.gpb + 2))
                        mm(PX[:, 0:T], wn0[:, :], xnT[:, b * T:(b + 1) * T], start=True, stop=False,
                           skip_group_check=True)
                        for i in range(TT):
                            m = mm(PX[:, i * P:(i + 1) * P], nmS[:, b, i, :], ident[:, :], start=False, stop=(i == 1),
                                   skip_group_check=True)
                        m.then_inc(S["L0nul"], 1)
                    elif phase == 1:
                        pe.wait_ge(S["L0rr"], at("L0rr", b + 1))
                        for q in range(4):
                            dst = PX if q % 2 == 0 else OB[1]
                            if q >= 2:
                                pe.wait_ge(S["L0rm"], at("L0rm", 4 * b + q - 1))
                            for k in range(2):
                                m = mm(dst[:, k * T:(k + 1) * T], w["sel0"][:, (2 * q + k) * P:(2 * q + k + 1) * P],
                                       rr[:, :], start=(k == 0), stop=(k == 1), skip_group_check=True)
                            m.then_inc(S["L0r"], 1)
                    elif phase == 2:
                        pe.wait_ge(S["L0rm"], at("L0rm", 4 * b + 4))
                        for i in range(TT):
                            dst = PX[:, i * P:(i + 1) * P]
                            for q in range(H0 // 2):
                                mm(dst, oT0[:, q, i * P:(i + 1) * P], w["wout0"][:, q * D:(q + 1) * D],
                                   start=(i == q == 0), stop=False, skip_group_check=True)
                            m = mm(dst, pn[:, i * P:(i + 1) * P], nvw[:, :], start=False, stop=True,
                                   skip_group_check=True)
                        m.then_inc(S["L0y"], 1)

                def finish(a, b, phase):
                    n = a.name
                    if phase == 0:
                        pe.wait_ge(S[n + "oe"], at(n + "oe", b + 1))
                        if b:
                            pe.wait_ge(S[n + "yx"], at(n + "yx", b))
                        for i in range(TT):
                            for s in range(2):
                                m = pe.transpose(OB[1][:, (2 * i + s) * P:(2 * i + s + 1) * P],
                                                 oe[:, s * T + i * P:s * T + (i + 1) * P], ident[:, :])
                        m.then_inc(S[n + "tn"], 1)
                    elif phase == 1:
                        pe.wait_ge(S[n + "on"], at(n + "on", b + 1))
                        for k in range(NT):
                            m = pe.transpose(OB[1][:, k * P:(k + 1) * P], on[:, k, :], ident[:, :])
                        m.then_inc(S[n + "tb"], 1)
                    else:
                        pe.wait_ge(S[n + "ont"], at(n + "ont", b + 1))
                        wo = w["wp2"] if a is A2 else w["wo3"]
                        for i in range(TT):
                            dst = OB[1][:, i * P:(i + 1) * P]
                            if a is A3:
                                mm(dst, xnT[:, b * T + i * P:b * T + (i + 1) * P], w["wox3"][:, :],
                                   start=(i == 0), stop=False, skip_group_check=True)
                            for s in range(2):
                                m = mm(dst, ont[:, 2 * i + s, :], wo[:, s * D:(s + 1) * D],
                                       start=(a is A2 and i == s == 0), stop=(s == 1), skip_group_check=True)
                        m.then_inc(S[n + "y"], 1)

                def attention(a, project, before, tail):
                    for step, u, n in order(a):
                        if step == "project":
                            project(u, n)
                        elif step == "scores":
                            scores(a, u, n)
                        elif step == "before":
                            before()
                        elif step == "turn":
                            turn_maxima(a, u)
                        elif step == "exp":
                            scores_T(a, u, n // GH, n % GH)
                        elif step == "values":
                            values(a, u, n)
                        elif step == "tail":
                            tail(u, n)

                def value0(n):
                    b, j, f = n // 4, n // 2 % 2, n % 2
                    if n >= 2:
                        pe.wait_ge(S["L0ve"], at("L0ve", n - 1))
                    for k in range(2):
                        m = mm(TB[n % 2][:, :], ctxT[:, k, b, j * P:(j + 1) * P],
                               w["wv0"][:, k * H0 * D0 + f * 512:k * H0 * D0 + (f + 1) * 512],
                               start=(k == 0), stop=(k == 1))
                    m.then_inc(S["L0v"], 1)

                def before0():
                    depool_1()
                    value0(2)
                    value0(3)
                    depool_2()
                    value0(4)
                    value0(5)
                    depool_3()
                    value0(6)
                    value0(7)
                    pe.wait_ge(S["L0ve"], at("L0ve", 8))
                    pe.wait_ge(S["p_pds"], at("p_pds"))

                def values2():
                    for n in range(NT):
                        m = mm(TB[0][:, n * P:(n + 1) * P], xnT[:, n * P:(n + 1) * P], w["wv2"][:, :],
                               start=(n == 0), stop=True, skip_group_check=True)
                    m.then_inc(S["L2v"], 1)
                    pe.wait_ge(S["L2ve"], at("L2ve", 4))
                    pe.wait_ge(S["L2ext"], at("L2ext"))

                def values3():
                    for n in range(NT):
                        for k in range(2):
                            m = mm(TB[0][:, n * P:(n + 1) * P], ctxT[:, k, n // TT, (n % TT) * P:(n % TT + 1) * P],
                                   w["wv3"][:, k * D:(k + 1) * D], start=(n == k == 0), stop=(k == 1),
                                   skip_group_check=True)
                    m.then_inc(S["L3v"], 1)

                def tokens_by(lhs, wgt, dst, name):
                    for n in range(NT):
                        m = mm(dst[:, n * P:(n + 1) * P], lhs[:, n * P:(n + 1) * P], wgt, start=(n == 0), stop=True,
                               skip_group_check=True)
                    m.then_inc(S[name], 1)

                def route(part, n, rt_):
                    pe.wait_ge(S["xT"], at("xT", part + 1))
                    for k in range(NT):
                        m = mm(PJ[:, k * NE:(k + 1) * NE], xnT[:, k * P:(k + 1) * P], rt_[:, :], start=(k == 0),
                               stop=True, skip_group_check=True)
                    m.then_inc(S[n + "lg"], 1)

                def gate_bias(n, b2):
                    pe.wait_ge(S[n + "gate"], at(n + "gate"))
                    for k in range(NT):
                        m = pe.transpose(PX[0:NE, k * P:(k + 1) * P], gates[:, k, :], ident[:, :])
                    m.then_inc(S[n + "gt"], 1)
                    pe.wait_ge(S[n + "gts"], at(n + "gts"))
                    for k in range(NT):
                        m = mm(PJ[:, k * P:(k + 1) * P], gT[:, k * P:(k + 1) * P], b2, start=(k == 0), stop=True,
                               skip_group_check=True)
                    m.then_inc(S[n + "bias"], 1)

                pe.wait_ge(S["ctx_in"], at("ctx_in"))
                value0(0)
                value0(1)
                norm_transposes(0)
                pe.wait_ge(S["xT"], at("xT", 1))
                pe.wait_ge(S["L0init"], at("L0init"))
                attention(A0, project0, before0, finish0)
                norm_transposes(1)
                pe.wait_ge(S["w_late"], 16 * len(LATE))
                pe.wait_ge(S["f_k"], at("f_k"))
                mm(TB[0][:, :], w["wk"][:, :], xk, start=True, stop=True).then_inc(S["f_kp"], 1)
                pe.wait_ge(S["f_r"], at("f_r"))
                tokens_by(xr, w["wr"][:, :], SB_[0], "f_rp")
                pe.wait_ge(S["f_ka"], at("f_ka"))
                tokens_by(ka, w["wv"][:, :], SB_[1], "f_v")
                norm_transposes(2)
                pe.wait_ge(S["xT"], at("xT", 3))
                pe.wait_ge(S["L1w"], at("L1w"))
                tokens_by(xnT, win[:, :], SB_[0], "L1y")
                norm_transposes(3)
                pe.wait_ge(S["xT"], at("xT", 4))
                tokens_by(xnT, wc[:, :], SB_[1], "L1fy")
                norm_transposes(4)
                pe.wait_ge(S["xT"], at("xT", 5))
                pe.wait_ge(S["L2init"], at("L2init"))
                attention(A2, project2, values2, lambda b, phase: finish(A2, b, phase))
                norm_transposes(5)
                route(5, "L2", w["rt2"])

                def expert_out2(n):
                    e, f = n // FT2, n % FT2
                    pe.wait_ge(S["g_h"], at("g_h", n + 1))
                    if f == 0 and e >= 2:
                        pe.wait_ge(S["g_ty"], at("g_ty", e - 1))
                    for k in range(NT):
                        m = mm(OB[e % 2][:, k * P:(k + 1) * P], hb[:, n % 3, k * P:(k + 1) * P],
                               stream[:, e % 2, 2, f * P:(f + 1) * P], start=(f == 0 and k == 0), stop=(f == FT2 - 1),
                               skip_group_check=True)
                    m.then_inc(S["g_y"], 1)

                for n in range(NE * FT2):
                    e, f = n // FT2, n % FT2
                    if f == 0:
                        pe.wait_ge(S[f"w_in{e % 2}"], at(f"w_in{e % 2}", 16 * (e // 2 + 1)))
                    if n >= 2:
                        pe.wait_ge(S["g_gl"], at("g_gl", n - 1))
                    mm(SB_[n % 2][:, :], stream[:, e % 2, 1, f * P:(f + 1) * P], xnT[:, :], start=True, stop=True)\
                        .then_inc(S["g_zg"], 1)
                    if n >= 2:
                        pe.wait_ge(S["g_h"], at("g_h", n - 1))
                    mm(TB[n % 2][:, :], stream[:, e % 2, 0, f * P:(f + 1) * P], xnT[:, :], start=True, stop=True)\
                        .then_inc(S["g_z1"], 1)
                    if n == 1:
                        gate_bias("L2", w["b2e"][0:NE, :])
                    if n:
                        expert_out2(n - 1)
                expert_out2(NE * FT2 - 1)
                pe.wait_ge(S["L3init"], at("L3init"))
                values3()
                norm_transposes(6)
                pe.wait_ge(S["xT"], at("xT", 7))
                pe.wait_ge(S["L3mask"], at("L3mask"))
                attention(A3, project3, lambda: pe.wait_ge(S["L3ve"], at("L3ve")), lambda b, phase: finish(A3, b, phase))
                norm_transposes(7)
                route(7, "L3", w["rt3"])

                def expert_out3(n):
                    e, f = n // FT3, n % FT3
                    pe.wait_ge(S["h_h"], at("h_h", n + 1))
                    if f == 0 and e >= 2:
                        pe.wait_ge(S["h_ty"], at("h_ty", e - 1))
                    for k in range(NT):
                        m = mm(OB[e % 2][:, k * P:(k + 1) * P], hb[:, n % 3, k * P:(k + 1) * P],
                               w["fw2"][:, n * D:(n + 1) * D], start=(f == 0 and k == 0), stop=(f == FT3 - 1),
                               skip_group_check=True)
                    m.then_inc(S["h_y"], 1)

                for n in range(E3 * FT3):
                    if n >= 2:
                        pe.wait_ge(S["h_h"], at("h_h", n - 1))
                    mm(SB_[n % 2][:, :], w["fw1"][:, n * P:(n + 1) * P], xnT[:, :], start=True, stop=True)\
                        .then_inc(S["h_z"], 1)
                    if n == 1:
                        gate_bias("L3", w["fb2"][0:NE, :])
                    if n:
                        expert_out3(n - 1)
                expert_out3(E3 * FT3 - 1)

        @block.scalar
        def _(act):
            f = nc.scalar.activation
            act.wait_ge(S["pre_pe"], 3)
            f(wcomb[:, :], bank[2][:, 0:D], ACT.Copy).then_inc(S["pre_act"], 1)
            with act.Fori(0, PAIRS) as it:
                regs = turn(act, it)

                def at(name, n=None):
                    return count(act, regs, name, n)

                def norm_out(part):
                    act.wait_ge(S["tr"], at("tr", part + 1))
                    f(xnT[:, :], PX[:, :], ACT.Copy).then_inc(S["xT"], 1)

                def turned(a, u):
                    act.wait_ge(S[a.name + "mt"], at(a.name + "mt", u + 1))
                    if u:
                        act.wait_ge(S[a.name + "mrow"], at(a.name + "mrow", 16 * u))
                    f((mT if a is A0 else mTr)[:, :], PX[0:GH, 0:T], ACT.Copy).then_inc(S[a.name + "mte"], 1)

                def exps(a, u, n):
                    k = a.items * u + n
                    act.wait_ge(S[a.name + "st"], at(a.name + "st", k + 1))
                    j = a.halves * u + n // GH
                    if n % GH == 0 and j >= 2:
                        act.wait_ge(S[a.name + "pv"], at(a.name + "pv", j - 1))
                    f(pbuf[:, j % 2, n % GH, :], TB[k % 2][:, :], ACT.Exp, scale=a.scale).then_inc(S[a.name + "p"], 1)

                def take0(u, q):
                    n = 2 * u + q
                    act.wait_ge(S["L0proj"], at("L0proj", n + 1))
                    if u >= RING:
                        act.wait_ge(S["L0st"], at("L0st", A0.items * (u - RING + 1)))
                    for c in range(2):
                        f(qk0[0:D0, u % RING, 2 * q + c, :, 0:T],
                          PJ[64 * c:64 * c + 64, :].rearrange("p (k t) -> p k t", k=2), ACT.Copy)\
                            .then_inc(S["L0act"], 1)

                def take2(u, q):
                    gb = w["gb"]
                    n = 2 * u + q
                    act.wait_ge(S["L2proj"], at("L2proj", n + 1))
                    if n >= 2:
                        act.wait_ge(S["L2q"], at("L2q", GH * u)) if q == 0 else act.wait_ge(S["L2k"], at("L2k", u))
                    if q == 0:
                        f(bpart[0][:, 0:T], PJ[:, 0:T], ACT.Copy, scale=gb[:, 0:1]).then_inc(S["L2bp"], 1)
                    else:
                        f(bpart[1][:, :], PJ[:, :], ACT.Identity, scale=gb[:, 2:3], bias=gb[:, 8:9])\
                            .then_inc(S["L2bp"], 1)

                def take3(u, q):
                    gb = w["gb"]
                    n = 2 * u + q
                    masked = (tmp, tmp2)[n % 2]
                    act.wait_ge(S["L3tm"], at("L3tm", n + 1))
                    if n >= 2:
                        act.wait_ge(S["L3k"], at("L3k", n - 1))
                    f(bpart[n % 2][:, 0:T], masked[:, 0:T], ACT.Copy, scale=gb[:, 4:5])
                    f(bpart[n % 2][:, T:2 * T], masked[:, T:2 * T], ACT.Copy, scale=gb[:, 6:7])\
                        .then_inc(S["L3bp"], 1)

                def attention(a, take, before, tail):
                    for step, u, n in order(a):
                        if step == "take":
                            take(u, n)
                        elif step == "before":
                            before()
                        elif step == "turn":
                            turned(a, u)
                        elif step == "exp":
                            exps(a, u, n)
                        elif step == "tail":
                            tail(u, n)

                def value0_out(n):
                    act.wait_ge(S["L0v"], at("L0v", n + 1))
                    b, j, h = n // 4, n // 2 % 2, n % 2
                    if n:
                        act.wait_ge(S["L0ve"], at("L0ve", n))
                    f(v0[:, b, j, h * 512:(h + 1) * 512], TB[n % 2][:, :], ACT.Copy).then_inc(S["L0ve"], 1)

                def before0():
                    act.wait_ge(S["p_dep"], at("p_dep"))
                    f(dep, four(OB[0][:, :]), ACT.Copy).then_inc(S["p_deps"], 1)
                    for n in (2, 4, 6):
                        value0_out(n)

                def v2_out():
                    act.wait_ge(S["L2v"], at("L2v"))
                    for b in range(2):
                        for k in range(2):
                            dst = v2[:, b, 2:4, :, 9 * k:9 * k + D2].rearrange("p j (s k c) d -> p j s k c d", s=2, k=2)[:, :, :, k]
                            src = TB[0][:, b * T:(b + 1) * T].rearrange("p (j s k c d) -> p j s k c d", j=2, s=2, k=2, c=4)[:, :, :, k]
                            f(dst.rearrange("p j s c d -> p (j s) c d"), src.rearrange("p j s c d -> p (j s) c d"),
                              ACT.Copy).then_inc(S["L2ve"], 1)

                def tail0(b, phase):
                    if phase:
                        return
                    act.wait_ge(S["L0nul"], at("L0nul", b + 1))
                    if b:
                        act.wait_ge(S["L0y"], at("L0y", b))
                    f(pn[:, :], PX[:, 0:T], ACT.Exp, scale=A0.scale).then_inc(S["L0pn"], 1)

                def tail(a):
                    n = a.name

                    def run(b, phase):
                        if phase == 0:
                            act.wait_ge(S[n + "pv"], at(n + "pv", a.halves * a.gpb * (b + 1)))
                            f(oe, OB[0][:, :], ACT.Copy).then_inc(S[n + "oe"], 1)
                        if phase == 1:
                            act.wait_ge(S[n + "tb"], at(n + "tb", b + 1))
                            f(ont, four(OB[1][:, :]), ACT.Copy).then_inc(S[n + "ont"], 1)
                    return run

                act.wait_ge(S["ctx_in"], at("ctx_in"))
                for n, unused in enumerate((xnT[:, 0:CTX], xnT[:, CTX:2 * CTX], pn[:, :], rr[:, :])):
                    m = f(unused, ctxN[:, n, :], ACT.Square, accum_out=ss[:, n:n + 1])
                m.then_inc(S["p_ss"], 1)
                act.wait_ge(S["p_ss"], at("p_ss"))
                value0_out(0)
                norm_out(0)
                attention(A0, take0, before0, tail0)
                norm_out(1)
                act.wait_ge(S["xT"], at("xT", 2))
                act.wait_ge(S["f_0"], at("f_0"))
                for k in range(2):
                    m = f(hb[:, k, :].rearrange("p (b t) -> p b t", b=2)[:, :, 1:T],
                          xnT[:, :].rearrange("p (b t) -> p b t", b=2)[:, :, 0:T - 1], ACT.Copy, scale=om[:, k:k + 1])
                m.then_inc(S["f_a"], 1)
                act.wait_ge(S["f_rp"], at("f_rp"))
                f(tmp[:, :], SB_[0][:, :], ACT.Tanh, scale=0.5).then_inc(S["f_th"], 1)
                norm_out(2)
                norm_out(3)
                act.wait_ge(S["L1fb"], at("L1fb"))
                f(tmp2[:, :], tmp[:, :], ACT.Tanh).then_inc(S["L1ft"], 1)
                norm_out(4)
                attention(A2, take2, v2_out, tail(A2))
                norm_out(5)

                def route(n):
                    act.wait_ge(S[n + "dl"], at(n + "dl"))
                    f(ex[:, :, :], lg[:, :, :], ACT.Exp).then_inc(S[n + "ex"], 1)

                def gates_out(n):
                    act.wait_ge(S[n + "gt"], at(n + "gt"))
                    f(gT[:, :], PX[0:NE, :], ACT.Copy).then_inc(S[n + "gts"], 1)

                route("L2")
                for n in range(NE * FT2):
                    act.wait_ge(S["g_zg"], at("g_zg", n + 1))
                    if n >= 2:
                        act.wait_ge(S["g_h"], at("g_h", n - 1))
                    f(gl[:, n % 2, :], SB_[n % 2][:, :], ACT.Gelu, bias=w["bg2"][:, n:n + 1]).then_inc(S["g_gl"], 1)
                    if n == 1:
                        gates_out("L2")
                norm_out(6)
                attention(A3, take3, lambda: None, tail(A3))
                norm_out(7)
                route("L3")
                for n in range(E3 * FT3):
                    act.wait_ge(S["h_z"], at("h_z", n + 1))
                    if n >= 3:
                        act.wait_ge(S["h_y"], at("h_y", n - 2))
                    f(hb[:, n % 3, :], SB_[n % 2][:, :], ACT.Gelu, bias=w["fb1"][:, n:n + 1]).then_inc(S["h_h"], 1)
                    if n == 1:
                        gates_out("L3")

        @block.vector
        def _(dve):
            v = nc.vector
            made["dve"] = 0

            pre = S["pre_dve"]
            dve.wait_ge(S["rows"], 16 * len(ROWS))
            dve.wait_ge(S["pl"], 16)
            v.tensor_copy(plf[:, :, :], pli[:, :, :]).then_inc(pre, 1)
            v.memset(oneb[:, :], 1.0)
            v.memset(wn0[:, :], 0.0)
            v.memset(nmS[:, :, :, :], 0.0)
            v.memset(on[:, :, :], 0.0)
            v.memset(half[:, :], -0.5).then_inc(pre, 1)
            dve.wait_ge(S["w_early"], 16 * len(EARLY))
            v.tensor_tensor(wnt[:, :, :], w["wq0"][:, :].rearrange("p (h d) -> p h d", h=H0),
                            r["nk"][:, None, :].broadcast_to([P, H0, D0]), ALU.mult).then_inc(pre, 1)
            dve.wait_ge(pre, 3)
            v.tensor_reduce(wnr[:, :], wnt[:, :, :], AX.X, ALU.add).then_inc(pre, 1)
            dve.wait_ge(pre, 4)
            v.tensor_copy(wn0[:, :].rearrange("p (c u) -> p u c", c=GH)[:, 0:GH, :],
                          wnr[:, :].rearrange("p (u c) -> p u c", c=GH))
            v.tensor_copy(trib[:, :, :], w["tri"][:, :].rearrange("p (a t) -> p a t", a=2)).then_inc(pre, 1)
            dve.wait_ge(S["pre_pe"], 1)
            for p in range(2):
                v.tensor_scalar(cum[:, 0, :, p::2], bank[0][:, p * B:(p + 1) * B].rearrange("p (i b) -> p i b", b=2),
                                -1.0, None, ALU.add).then_inc(pre, 1)
            dve.wait_ge(pre, 7)
            v.tensor_scalar(cum[:, 1, :, :], cum[:, 0, :, :], float(T), None, ALU.add).then_inc(pre, 1)
            dve.wait_ge(S["pre_pe"], 2)
            v.tensor_copy(nvw[:, :], bank[1][:, 0:D])
            dve.wait_ge(S["pre_pe"], 4)
            v.tensor_copy(wc[:, :], bank[3][:, 0:D]).then_inc(pre, 1)
            dve.wait_ge(pre, 9)

            with dve.Fori(0, PAIRS) as it:
                regs = turn(dve, it)

                def at_cut(name, n=None):
                    return count(dve, regs, name, n, cut=True)

                def at(name, n=None):
                    return count(dve, regs, name, n)

                def mark(ins):
                    made["dve"] += 1
                    ins.then_inc(S["dve"], 1)
                    return made["dve"]

                def after(k):
                    dve.wait_ge(S["dve"], at_cut("dve", k))

                def link(ins):
                    after(mark(ins))

                def norm(part, src):
                    for n in range(NT):
                        k = mark(v.bn_stats(st6[:, n, :], src[:, n, :]))
                    after(k)
                    for n in range(NT):
                        m = v.bn_aggr(mv[:, n, :], st6[:, n, :])
                    m.then_inc(S["mv"], 1)
                    dve.wait_ge(S["rs"], at("rs", part + 1))
                    for n in range(NT):
                        v.tensor_scalar(xn[:, n, :], src[:, n, :], mv[:, n, 0:1], rs[:, n:n + 1], ALU.subtract,
                                        ALU.mult).then_inc(S["xn"], 1)
                    dve.wait_ge(S["xn"], at_cut("xn", NT * (part + 1)))

                def maxima(a, u, c):
                    for i in range(TT):
                        n = 8 * u + TT * c + i
                        dve.wait_ge(S[a.name + "score"], at(a.name + "score", n + 1))
                        if a is A0:
                            dst = nmS[:, u // a.gpb, i, 32 * c + u % a.gpb:32 * c + u % a.gpb + 1]
                            width = T + 2
                        else:
                            if u >= 2 and c == i == 0:
                                dve.wait_ge(S[a.name + "mt"], at(a.name + "mt", u - 1))
                            dst = nm[:, u % 2, i, c:c + 1]
                            width = 2 * T if a is A2 else T
                        v.tensor_reduce(dst, SB_[n % 2][:, 0:width], AX.X, ALU.max, negate=True)\
                            .then_inc(S[a.name + "max"], 1)

                def round0(u, q):
                    n = 2 * u + q
                    dve.wait_ge(S["L0act"], at("L0act", 2 * (n + 1)))
                    if n == 0:
                        dve.wait_ge(S["L0init"], at("L0init"))
                    if u >= 2:
                        dve.wait_ge(S["L0score"], at("L0score", 8 * (u - 1)))
                    v.tensor_copy(qkr0[:, u % 2, q, :, 0:T], PJ[:, :].rearrange("p (k t) -> p k t", k=2))\
                        .then_inc(S["L0qkr"], 1)

                def q_low(q_, c, rows, x_, scale, high, signal):
                    v.scalar_tensor_tensor(q_[rows, c, :], x_[rows, 0:T], scale[rows, :], high[rows, 0:T].bitcast(F32),
                                           ALU.mult, ALU.add).then_inc(S[signal], 1)

                def split2(u, q):
                    gb = w["gb"]
                    dve.wait_ge(S["L2bp"], at("L2bp", 2 * u + q + 1))
                    if u >= RING:
                        dve.wait_ge(S["L2st"], at("L2st", A2.items * (u - RING + 1)))
                    if q == 0:
                        for c in range(GH):
                            q_low(q2[:, u % RING], c, slice(SLOT2 * c, SLOT2 * (c + 1)), PJ, gb[:, 1:2], bpart[0], "L2q")
                    else:
                        v.scalar_tensor_tensor(k2[:, u % RING, :], PJ[:, :], gb[:, 3:4], bpart[1][:, :].bitcast(F32),
                                               ALU.mult, ALU.add).then_inc(S["L2k"], 1)

                def mask3(u, q):
                    b, n = u // A3.gpb, 2 * u + q
                    s = 2 * (u % A3.gpb) + q
                    masked = (tmp, tmp2)[n % 2]
                    dve.wait_ge(S["L3proj"], at("L3proj", n + 1))
                    if n >= 2:
                        dve.wait_ge(S["L3q"], at("L3q", 2 * n - 2))
                    v.scalar_tensor_tensor(masked[:, 0:T], PJ[:, 0:T], w["bq3"][:, s:s + 1], mqk[:, b, 0, :], ALU.add,
                                           ALU.mult)
                    v.scalar_tensor_tensor(masked[:, T:2 * T], PJ[:, T:2 * T], w["bk3"][:, s:s + 1], mqk[:, b, 1, :],
                                           ALU.add, ALU.mult).then_inc(S["L3tm"], 1)

                def split3(u, q):
                    gb = w["gb"]
                    n = 2 * u + q
                    masked = (tmp, tmp2)[n % 2]
                    dve.wait_ge(S["L3bp"], at("L3bp", n + 1))
                    if u >= RING:
                        dve.wait_ge(S["L3st"], at("L3st", A3.items * (u - RING + 1)))
                    v.scalar_tensor_tensor(k3[:, u % RING, q, :], masked[:, T:2 * T], gb[:, 7:8],
                                           bpart[n % 2][:, T:2 * T].bitcast(F32), ALU.mult, ALU.add)\
                        .then_inc(S["L3k"], 1)
                    for c in range(2):
                        q_low(q3[:, u % RING], 2 * q + c, slice(SLOT3 * c, SLOT3 * (c + 1)), masked, gb[:, 5:6],
                              bpart[n % 2], "L3q")

                def attention(a, take, split, before, out, tail):
                    for step, u, n in order(a):
                        if step == "take":
                            take(u, n)
                        elif step == "split":
                            split(u, n)
                        elif step == "scores":
                            maxima(a, u, n)
                        elif step == "before":
                            before()
                        elif step == "values":
                            out(u)
                        elif step == "tail":
                            tail(u, n)

                def value0_out(n):
                    dve.wait_ge(S["L0v"], at("L0v", n + 1))
                    dve.wait_ge(S["L0ve"], at("L0ve", n))
                    b, j, h = n // 4, n // 2 % 2, n % 2
                    v.tensor_copy(v0[:, b, j, h * 512:(h + 1) * 512], TB[n % 2][:, :]).then_inc(S["L0ve"], 1)

                def before0():
                    dve.wait_ge(S["p_bd"], at("p_bd"))
                    v.tensor_scalar(bds[:, :, :], four(SB_[0][:, :]), 1.0, None, ALU.min).then_inc(S["p_bds"], 1)
                    value0_out(3)
                    dve.wait_ge(S["p_pb"], at("p_pb"))
                    link(v.tensor_scalar(tmp[:, :], SB_[1][:, :], -1.0, 0.0, ALU.add, ALU.max))
                    for s in range(TT):
                        m = v.tensor_scalar(gsel[:, s, :, :], tmp[:, :].rearrange("p (b t) -> p b t", b=2),
                                            float(T - 1), w["srow"][:, s:s + 1], ALU.min, ALU.is_equal)
                    m.then_inc(S["p_g"], 1)
                    value0_out(5)
                    dve.wait_ge(S["p_pd"], at("p_pd"))
                    v.tensor_tensor(pdb[:, :, :], four(OB[1][:, :]), r["bin"][:, None, :].broadcast_to([P, NT, D]),
                                    ALU.add).then_inc(S["p_pds"], 1)
                    value0_out(7)

                def out0(u):
                    dve.wait_ge(S["L0o"], at("L0o", u + 1))
                    if u == A0.gpb:
                        dve.wait_ge(S["L0y"], at("L0y", 1))
                    g = u % A0.gpb
                    v.tensor_copy(oT0[:, 2 * g:2 * g + 2, :], OB[0][:, :].rearrange("p (k t) -> p k t", k=2))\
                        .then_inc(S["L0oe"], 1)

                def tail0(b, phase):
                    if phase == 0:
                        dve.wait_ge(S["L0pn"], at("L0pn", b + 1))
                        dve.wait_ge(S["L0pv"], at("L0pv", A0.gpb * (b + 1)))
                        if b:
                            dve.wait_ge(S["L0r"], at("L0r", 4 * b))
                        link(v.tensor_tensor(rr[:, :], OB[1][:, 0:T], pn[:, :], ALU.add))
                        link(v.reciprocal(rr[:, :], rr[:, :]))
                        v.tensor_tensor(pn[:, :], pn[:, :], rr[:, :], ALU.mult).then_inc(S["L0rr"], 1)
                    elif phase == 1:
                        dve.wait_ge(S["L0oe"], at("L0oe", A0.gpb * (b + 1)))
                        for q in range(4):
                            dve.wait_ge(S["L0r"], at("L0r", 4 * b + q + 1))
                            src = PX if q % 2 == 0 else OB[1]
                            o = oT0[:, 2 * q:2 * q + 2, :]
                            v.tensor_tensor(o, src[:, :].rearrange("p (k t) -> p k t", k=2), o, ALU.mult)\
                                .then_inc(S["L0rm"], 1)
                    elif phase == 2:
                        dve.wait_ge(S["L0y"], at("L0y", b + 1))
                        for i in range(TT):
                            k = mark(v.bn_stats(st6[:, i, :], PX[:, i * P:(i + 1) * P]))
                        after(k)
                        for i in range(TT):
                            m = v.bn_aggr(mv[:, i, :], st6[:, i, :])
                        m.then_inc(S["L0ys"], 1)
                    else:
                        dve.wait_ge(S["L0yr"], at("L0yr", b + 1))
                        for i in range(TT):
                            xt = x[:, b * TT + i, :]
                            link(v.tensor_scalar(xt, PX[:, i * P:(i + 1) * P], mv[:, i, 0:1], rs[:, i:i + 1],
                                                 ALU.subtract, ALU.mult))
                            link(v.tensor_tensor(xt, xt, r["ls0"][:, :], ALU.mult))
                            m = v.tensor_tensor(xt, xt, xb[:, b * TT + i, :], ALU.add)
                        m.then_inc(S["L0yx"], 1)

                def tail(a):
                    n = a.name

                    def output(b):
                        dve.wait_ge(S[n + "y"], at(n + "y", b + 1))
                        if b == 0:
                            dve.wait_ge(S[n + "xb"], at(n + "xb"))
                        xs = x[:, b * TT:(b + 1) * TT, :]
                        m = v.tensor_tensor(xs, OB[1][:, 0:T].rearrange("p (i d) -> p i d", i=TT),
                                            xb[:, b * TT:(b + 1) * TT, :], ALU.add)
                        m.then_inc(S[n + "yx"], 1)

                    def run(b, phase):
                        if phase == 1:
                            return
                        if phase == 2:
                            output(b)
                            return
                        dve.wait_ge(S[n + "tn"], at(n + "tn", b + 1))
                        if a is A2:
                            px = OB[1][:, :].rearrange("p (g w) -> p g w", w=32)[:, :, 0:18].rearrange("p g (k w) -> p g k w", k=2)
                            o = on[:, :, :].rearrange("p n (c w) -> p (n c) w", w=32)[:, :, 0:18].rearrange("p g (k w) -> p g k w", k=2)
                            rc = rr[:, 0:32].rearrange("p (g k w) -> p g k w", k=2, w=1)
                            link(v.reciprocal(rc, px[:, :, :, D2:D2 + 1]))
                            v.tensor_tensor(o, px, rc.broadcast_to([P, 16, 2, D2 + 1]), ALU.mult).then_inc(S[n + "on"], 1)
                        else:
                            px = OB[1][:, :].rearrange("p (g w) -> p g w", w=32)[:, :, 0:D3 + 1]
                            o = on[:, :, :].rearrange("p n (c w) -> p (n c) w", w=32)[:, :, 0:D3 + 1]
                            rc = rr[:, 0:16].rearrange("p (g w) -> p g w", w=1)
                            link(v.reciprocal(rc, px[:, :, D3:D3 + 1]))
                            v.tensor_tensor(o, px, rc.broadcast_to([P, 16, D3 + 1]), ALU.mult).then_inc(S[n + "on"], 1)
                    return run

                def v3_out():
                    dve.wait_ge(S["L3v"], at("L3v"))
                    v.tensor_tensor(gl[:, 0, :].rearrange("p (n d) -> p n d", n=NT), four(TB[0][:, :]),
                                    r["bv3"][:, None, :].broadcast_to([P, NT, D]), ALU.add).then_inc(S["L3vt"], 1)
                    dve.wait_ge(S["ctx_in"], at("ctx_in"))
                    dve.wait_ge(S["L3init"], at("L3init"))
                    dve.wait_ge(S["L3vt"], at_cut("L3vt"))
                    for n in range(NT):
                        m = v.tensor_scalar(v3[:, n // TT, n % TT, :, 0:D3],
                                            gl[:, 0, n * D:(n + 1) * D].rearrange("p (h d) -> p h d", h=H3),
                                            maskC[:, n:n + 1], None, ALU.mult)
                    m.then_inc(S["L3ve"], 1)

                dve.wait_ge(S["x_in"], at("x_in"))
                norm(0, xin)
                link(v.tensor_copy(cc[:, :, :], cum[:, :, bass.ds(it, 1), :].rearrange("p a i n -> p a (i n)")))
                for n in range(NT):
                    k = mark(v.tensor_scalar(eqb[:, n // 2, n % 2, :], w["iota"][:, :], cc[:, 0, n:n + 1], None, ALU.is_equal))
                after(k)
                for n in range(NT):
                    m = v.scalar_tensor_tensor(eqb[:, n // 2, n % 2, :], w["iota"][:, :], cc[:, 1, n:n + 1],
                                               eqb[:, n // 2, n % 2, :], ALU.is_equal, ALU.add)
                m.then_inc(S["p_eq"], 1)
                dve.wait_ge(S["p_rp"], at("p_rp"))
                for n in range(NT):
                    m = v.scalar_tensor_tensor(hps[:, n, :], ctxN[:, n, 0:D], ss[:, n:n + 1], r["ginit"][:, :],
                                               ALU.mult, ALU.mult)
                m.then_inc(S["p_hp"], 1)
                value0_out(1)
                dve.wait_ge(S["xlb"], at("xlb"))
                attention(A0, round0, lambda u, q: None, before0, out0, tail0)
                dve.wait_ge(S["L0yx"], at("L0yx"))
                norm(1, x)
                dve.wait_ge(S["f_a"], at("f_a"))
                mu = w["mu"]
                v.scalar_tensor_tensor(xk, xnT[:, :], mu[:, 1:2], hb[:, 1, :], ALU.mult, ALU.add).then_inc(S["f_k"], 1)
                v.scalar_tensor_tensor(xr, xnT[:, :], mu[:, 0:1], hb[:, 0, :], ALU.mult, ALU.add).then_inc(S["f_r"], 1)
                dve.wait_ge(S["f_kp"], at("f_kp"))
                link(v.tensor_scalar(tmp2[:, :], TB[0][:, :], 0.0, None, ALU.max))
                v.tensor_tensor(ka, tmp2[:, :], tmp2[:, :], ALU.mult).then_inc(S["f_ka"], 1)
                dve.wait_ge(S["f_v"], at("f_v"))
                dve.wait_ge(S["f_th"], at("f_th"))
                link(v.scalar_tensor_tensor(four(hb[:, 0, :]), four(tmp[:, :]), 1.0, four(SB_[1][:, :]), ALU.add, ALU.mult))
                link(v.scalar_tensor_tensor(x[:, :, :], four(hb[:, 0, :]), 0.5, x[:, :, :], ALU.mult, ALU.add))
                v.tensor_scalar(win[:, :], w["win"][:, :], w["gres"][:, 0:1], None, ALU.mult).then_inc(S["L1w"], 1)
                norm(2, x)
                link(v.tensor_tensor(x[:, :, :], x[:, :, :], pdb[:, :, :], ALU.add))
                dve.wait_ge(S["L1y"], at("L1y"))
                link(v.tensor_tensor(x[:, :, :], four(SB_[0][:, :]), x[:, :, :], ALU.add))
                norm(3, x)
                dve.wait_ge(S["L1fy"], at("L1fy"))
                v.tensor_tensor(four(tmp[:, :]), four(SB_[1][:, :]), r["bff1"][:, None, :].broadcast_to([P, NT, D]), ALU.add)\
                    .then_inc(S["L1fb"], 1)
                dve.wait_ge(S["L1ft"], at("L1ft"))
                link(v.tensor_tensor(x[:, :, :], four(tmp2[:, :]), x[:, :, :], ALU.add))
                norm(4, x)
                attention(A2, split2, lambda u, q: None, lambda: None, lambda u: None, tail(A2))
                dve.wait_ge(S["L2yx"], at("L2yx"))
                norm(5, x)

                def route(n, bias):
                    dve.wait_ge(S[n + "lg"], at(n + "lg"))
                    src = PJ[:, 0:NT * NE].rearrange("p (n e) -> p n e", n=NT)
                    if bias is None:
                        link(v.tensor_copy(lg[:, :, :], src))
                    else:
                        link(v.tensor_tensor(lg[:, :, :], src, bias[:, None, :].broadcast_to([P, NT, NE]), ALU.add))
                    link(v.tensor_reduce(r4[:, 0, :], lg[:, :, :], AX.X, ALU.max))
                    v.tensor_tensor(lg[:, :, :], lg[:, :, :], r4[:, 0, :, None].broadcast_to([P, NT, NE]), ALU.subtract)\
                        .then_inc(S[n + "dl"], 1)
                    dve.wait_ge(S[n + "ex"], at(n + "ex"))
                    link(v.tensor_reduce(r4[:, 0, :], ex[:, :, :], AX.X, ALU.add))
                    link(v.reciprocal(r4[:, 1, :], r4[:, 0, :]))
                    link(v.tensor_tensor(pr[:, :, :], ex[:, :, :], r4[:, 1, :, None].broadcast_to([P, NT, NE]), ALU.mult))
                    of = pr[:, :, :, None].broadcast_to([P, NT, NE, NE])
                    other = pr[:, :, None, :].broadcast_to([P, NT, NE, NE])
                    link(v.tensor_tensor(rank[:, :, :, :], other, of, ALU.is_gt))
                    link(v.tensor_tensor(rank2[:, :, :, :], other, of, ALU.is_equal))
                    before = w["etri"][:, :].rearrange("p (a b) -> p a b", a=NE)[:, None, :, :].broadcast_to([P, NT, NE, NE])
                    link(v.tensor_tensor(rank2[:, :, :, :], rank2[:, :, :, :], before, ALU.mult))
                    link(v.tensor_tensor(rank[:, :, :, :], rank[:, :, :, :], rank2[:, :, :, :], ALU.add))
                    link(v.tensor_reduce(lg[:, :, :], rank[:, :, :, :], AX.X, ALU.add))
                    v.scalar_tensor_tensor(gates[:, :, :], lg[:, :, :], 2.0, pr[:, :, :], ALU.is_lt, ALU.mult)\
                        .then_inc(S[n + "gate"], 1)

                route("L2", None)

                def weigh(n, e, bank_, sem_y, y_n, sem_ty, sem_acc, gated=True):
                    dve.wait_ge(S[sem_y], at(sem_y, y_n))
                    if e >= 2:
                        dve.wait_ge(S[sem_acc], at(sem_acc, e - 1))
                    dst = (tmp, tmp2)[e % 2]
                    if gated:
                        m = v.tensor_tensor(four(dst[:, :]), four(bank_[:, :]),
                                            gates[:, :, e:e + 1].broadcast_to([P, NT, D]), ALU.mult)
                    else:
                        m = v.tensor_copy(dst[:, :], bank_[:, :])
                    m.then_inc(S[sem_ty], 1)

                for n in range(NE * FT2):
                    dve.wait_ge(S["g_z1"], at("g_z1", n + 1))
                    dve.wait_ge(S["g_gl"], at("g_gl", n + 1))
                    if n >= 3:
                        dve.wait_ge(S["g_y"], at("g_y", n - 2))
                    v.scalar_tensor_tensor(hb[:, n % 3, :], TB[n % 2][:, :], w["b12"][:, n:n + 1], gl[:, n % 2, :],
                                           ALU.add, ALU.mult).then_inc(S["g_h"], 1)
                    if n == 2:
                        dve.wait_ge(S["L2bias"], at("L2bias"))
                        v.tensor_tensor(x[:, :, :], four(PJ[:, :]), x[:, :, :], ALU.add).then_inc(S["L2acc0"], 1)
                    if n % FT2 == 1 and n > FT2:
                        e = n // FT2 - 1
                        weigh("L2", e, OB[e % 2], "g_y", FT2 * (e + 1), "g_ty", "g_acc")
                weigh("L2", NE - 1, OB[(NE - 1) % 2], "g_y", NE * FT2, "g_ty", "g_acc")
                dve.wait_ge(S["g_acc"], at("g_acc"))
                norm(6, x)
                v3_out()
                dve.wait_ge(S["L3mask"], at("L3mask"))
                attention(A3, mask3, split3, lambda: None, lambda u: None, tail(A3))
                dve.wait_ge(S["L3yx"], at("L3yx"))
                norm(7, x)
                route("L3", r["rb3"])
                for n in range(E3 * FT3):
                    if n == 2:
                        dve.wait_ge(S["L3bias"], at("L3bias"))
                        dve.wait_ge(S["sb2x"], at("sb2x"))
                        v.tensor_tensor(x[:, :, :], four(PJ[:, :]), xb[:, :, :], ALU.add).then_inc(S["L3acc0"], 1)
                    if n % FT3 == 1 and n > FT3:
                        e = n // FT3 - 1
                        weigh("L3", e, OB[e % 2], "h_y", FT3 * (e + 1), "h_ty", "h_acc", e < NE)
                weigh("L3", E3 - 1, OB[(E3 - 1) % 2], "h_y", E3 * FT3, "h_ty", "h_acc", False)

        @block.gpsimd
        def _(pool):
            g = nc.gpsimd
            made["pool"] = 0

            def bcast(row):
                return row[:, None, :].broadcast_to([P, NT, D])

            def pads0(behind):
                g.memset(qk0[0:D0, :, :, 0, T:T + 2], 0.0)
                for k in range(RING):
                    g.tensor_copy(qk0[0:D0, k, :, 1, T:T + 2], w["nkcol"][0:D0, :, None].broadcast_to([D0, GH, 2]))
                for k in range(2):
                    m = g.tensor_copy(qkr0[:, k, :, 1, T:T + 2], w["nkcol"][:, :, None].broadcast_to([P, 2, 2]))
                behind(m)
                g.memset(qk0[D0:D0 + 1, :, :, 1, :], 1.0).then_inc(S["L0init"], 1)

            pool.wait_ge(S["w_early"], 16 * len(EARLY))
            pool.wait_ge(S["rows"], 16 * len(ROWS))
            pool.wait_ge(S["pre_dve"], 9)

            def first(ins):
                ins.then_inc(S["pre_pool"], 1)
                pool.wait_ge(S["pre_pool"], 1)

            g.memset(om[:, :], 0.0).then_inc(S["stored"], 16)
            pool.wait_ge(S["stored"], 16)
            pads0(first)
            pool.wait_ge(S["L0init"], 1)
            with pool.Fori(0, PAIRS) as it:
                regs = turn(pool, it)

                def at(name, n=None):
                    return count(pool, regs, name, n, cut=True)

                def link(ins):
                    made["pool"] += 1
                    ins.then_inc(S["pool"], 1)
                    pool.wait_ge(S["pool"], at("pool", made["pool"]))

                def inv_std(src, dst, scale, eps, signal, k=1):
                    n = dst.shape[1]
                    link(g.tensor_scalar(rt[:, 0:n], src, scale, eps, ALU.mult, ALU.add))
                    g.tensor_tensor(dst, rt[:, 0:n], half[:, 0:n], ALU.pow).then_inc(S[signal], 1)
                    pool.wait_ge(S[signal], at(signal, k))

                def norm(part, scale=1.0, eps=EPS):
                    pool.wait_ge(S["mv"], at("mv", part + 1))
                    inv_std(mv[:, :, 1], rs[:, :], scale, eps, "rs", part + 1)

                def tail0(b):
                    pool.wait_ge(S["L0ys"], at("L0ys", b + 1))
                    inv_std(mv[:, 0:TT, 1], rs[:, 0:TT], 1.0, EPS_OUT, "L0yr", b + 1)

                def extra_keys():
                    for b in range(2):
                        for j in range(TT):
                            for k in range(2):
                                dst = v2[:, b, j, :, 9 * k:9 * k + D2].rearrange("p (s k c) d -> p s k c d", s=2, k=2)
                                src = ctxN[:, 2 * b + j, D:2 * D].rearrange("p (s k c d) -> p s k c d", s=2, k=2, c=GH)
                                m = g.tensor_copy(dst[:, :, k], src[:, :, k])
                    m.then_inc(S["L2ext"], 1)

                norm(0)
                pool.wait_ge(S["p_ss"], at("p_ss"))
                inv_std(ss[:, :], ss[:, :], 1.0 / CTX, EPS, "p_rp")
                pool.wait_ge(S["x_in"], at("x_in"))
                pool.wait_ge(S["stored"], at("stored"))
                g.tensor_tensor(xb[:, :, :], xin[:, :, :], bcast(r["lb0"]), ALU.add).then_inc(S["xlb"], 1)
                tail0(0)
                tail0(1)
                norm(1)
                pool.wait_ge(S["w_late"], 16 * len(LATE))
                g.tensor_scalar(om[:, :], w["mu"][:, :], -1.0, 1.0, ALU.mult, ALU.add)
                g.memset(hb[:, 0:2, :].rearrange("p k (b t) -> p k b t", b=2)[:, :, :, 0:1], 0.0).then_inc(S["f_0"], 1)
                pool.wait_ge(S["L0y"], at("L0y"))
                g.memset(q2[:, :, :, :].bitcast(F32), 0.0)
                norm(2, 1.0 + EPS, EPS * EPS)
                link(g.memset(v2[:, 0, :, :, :], 0.0))
                norm(3)
                link(g.memset(v2[:, 1, :, :, :], 0.0))
                v2s = v2[:, :, :, :, :].rearrange("p b j (s k c) w -> p (b j s) k c w", s=2, k=2)
                g.memset(v2s[:, :, 0, :, D2], 1.0)
                g.memset(v2s[:, :, 1, :, 2 * D2 + 1], 1.0).then_inc(S["L2init"], 1)
                extra_keys()
                norm(4)
                g.tensor_tensor(xb[:, :, :], x[:, :, :], bcast(r["bp2"]), ALU.add).then_inc(S["L2xb"], 1)
                g.memset(q3[:, :, :, :].bitcast(F32), 0.0)
                link(g.memset(v3[:, :, :, :, :], 0.0))
                g.memset(v3[:, :, :, :, D3:D3 + 1], 1.0).then_inc(S["L3init"], 1)
                norm(5)
                pool.wait_ge(S["ctx_in"], at("ctx_in"))
                for b in range(2):
                    mb = maskB[:, b * T:(b + 1) * T]
                    g.tensor_scalar(mqk[:, b, 0, :], mb, w["msel"][:, 0:1], w["msel"][:, 1:2], ALU.mult, ALU.add)
                    g.tensor_scalar(mqk[:, b, 1, :], mb, w["msel"][:, 0:1], w["msel"][:, 2:3], ALU.mult, ALU.add)
                    link(g.tensor_scalar(pn[:, :], mb, 0.0, w["msel"][:, 3:4], ALU.is_equal, ALU.mult))
                    link(g.tensor_tensor(mqk[:, b, 1, :], mqk[:, b, 1, :], pn[:, :], ALU.add))
                g.memset(om[:, 0:1], 0.0).then_inc(S["L3mask"], 1)
                pool.wait_ge(S["L2acc0"], at("L2acc0"))
                for e in range(NE):
                    pool.wait_ge(S["g_ty"], at("g_ty", e + 1))
                    if e:
                        pool.wait_ge(S["g_acc"], at("g_acc", e))
                    g.tensor_tensor(x[:, :, :], x[:, :, :], four((tmp, tmp2)[e % 2][:, :]), ALU.add).then_inc(S["g_acc"], 1)
                norm(6)
                g.tensor_tensor(xb[:, :, :], x[:, :, :], bcast(r["bo3"]), ALU.add).then_inc(S["L3xb"], 1)
                norm(7)
                link(g.tensor_tensor(xb[:, :, :], x[:, :, :], bcast(r["sb2"]), ALU.add))
                pool.wait_ge(S["L3y"], at("L3y"))
                pads0(link)
                pool.reg_add(regs[1], regs[0][1], 2)
                pool.wait_ge(S["L0init"], 1)
                pool.wait_ge(S["L0init"], regs[1])
                g.memset(om[:, 0:1], 0.0).then_inc(S["sb2x"], 1)
                pool.wait_ge(S["L3acc0"], at("L3acc0"))
                for e in range(E3):
                    pool.wait_ge(S["h_ty"], at("h_ty", e + 1))
                    if e:
                        pool.wait_ge(S["h_acc"], at("h_acc", e))
                    dst = x
                    if e == E3 - 1:
                        dst = xb
                    g.tensor_tensor(dst[:, :, :], x[:, :, :], four((tmp, tmp2)[e % 2][:, :]), ALU.add)\
                        .then_inc(S["h_acc"], 1)
                pool.wait_ge(S["h_acc"], at("h_acc"))
                g.memset(om[:, 1:2], 0.0).then_inc(S["x_out"], 1)

        return made


def layouts(a):
    f = lambda k: np.asarray(a[k])
    z = lambda *s: np.zeros(s, np.float32)
    d = {}
    d["x"] = f("x").reshape(PAIRS, 2, TT, P, D).transpose(0, 3, 1, 2, 4).reshape(PAIRS, P, NT * D)
    c = f("ctx_2048")
    d["ctxT"] = c.reshape(PAIRS, 2, T, 2, P).transpose(0, 4, 3, 1, 2).reshape(PAIRS, P, 4 * T)
    d["ctxN"] = c.reshape(PAIRS, 2, TT, P, CTX).transpose(0, 3, 1, 2, 4).reshape(PAIRS, P, NT * CTX)
    m = f("mask_BxS2_fk1")
    d["maskrow"] = m.reshape(PAIRS, 1, N)
    d["maskcol"] = m.reshape(PAIRS, 2, TT, P).transpose(0, 3, 1, 2).reshape(PAIRS, P, NT)
    d["pl"] = f("mask_BxS2_if0").reshape(B, 2, P).transpose(2, 1, 0).reshape(P, 2 * B)
    d["ident"] = np.eye(P, dtype=np.float32)
    i = np.arange(T)
    tri = (i[:, None] <= i[None, :]).astype(np.float32)
    d["tri"] = tri.reshape(2, P, T).transpose(1, 0, 2).reshape(P, 2 * T)
    step = 1e-3
    dt = -np.log(-np.expm1(-step))
    decay = np.exp(-step) * np.exp(-dt * np.maximum(i[None, :] - i[:, None], 0)) * tri
    d["decay"] = decay.astype(np.float32).reshape(2, P, T).transpose(1, 0, 2).reshape(P, 2 * T)
    d["iota"] = np.broadcast_to(i.astype(np.float32), (P, T))
    d["srow"] = i.astype(np.float32).reshape(2, P).T
    es = z(P, 4, 32)
    for u in range(4):
        es[:, u, u] = 1
    d["esum"] = es.reshape(P, P)
    d["wq0"] = f("L0_xattn_Wq")
    kv = f("L0_xattn_Wkv").reshape(2, P, 2, H0 * D0)
    d["wk0"] = kv[:, :, 0].transpose(1, 0, 2).reshape(P, -1)
    d["wv0"] = kv[:, :, 1].transpose(1, 0, 2).reshape(P, -1)
    null = f("L0_xattn_null_kv")
    nk = z(P, 1)
    nk[:D0, 0] = nk[D0:, 0] = null[0]
    d["nkcol"] = nk
    d["row_nk"] = null[0][None]
    nv, sel = z(2, D0, H0 // 2, P), z(P, H0 // 2, 2, D0)
    for h in range(H0):
        slot = 32 * (h % GH) + h // GH
        nv[h % 2, :, h // 2, slot] = null[1]
        sel[slot, h // 2, h % 2, :] = 1
    d["nullv"], d["sel0"] = nv.reshape(P, -1), sel.reshape(P, -1)
    d["wout0"] = f("L0_xattn_Wout").reshape(H0 // 2, P, D).transpose(1, 0, 2).reshape(P, -1)
    d["row_ls0"], d["row_lb0"] = f("L0_xattn_ln_scale")[None], f("L0_xattn_ln_bias")[None]
    d["wr"], d["wk"], d["wv"] = f("L0_ffn_W_r").T, f("L0_ffn_W_k").T, f("L0_ffn_W_v").T
    d["mu"] = np.stack([f("L0_ffn_mu_r"), f("L0_ffn_mu_k")], 1)
    d["win"], d["gres"] = f("L1_xattn_W_in").T, f("L1_xattn_g_res")[:, None]
    d["row_ginit"], d["row_bin"] = f("L1_xattn_g_init")[None, :D], f("L1_xattn_b_in")[None]
    d["wcT"], d["a1"], d["a2"] = f("L1_ffn_weight").T, f("L1_ffn_aux_weight1"), f("L1_ffn_aux_weight2")
    d["row_bff1"] = f("L1_ffn_bias")[None]
    qkv = f("L2_xattn_w_qkv")
    wq, wk, perm = z(P, 4, P), z(P, 4, P), z(P, 4, P)
    wp = z(P, 2, D)
    proj = f("L2_xattn_w_proj")
    gb = z(P, 9)
    gb[:, 0::2] = 1
    gb[:, 8] = 0
    gb[MROW, 8] = 1
    for h in range(H2):
        u, cc = h // GH, h % GH
        rows = slice(h * D2, (h + 1) * D2)
        for k in range(3):
            s = slice(SLOT2 * cc + k * D2, SLOT2 * cc + (k + 1) * D2)
            wq[:, u, s] = qkv[rows].T
            wk[:, u, s] = qkv[D + h * D2:D + (h + 1) * D2].T
            perm[rows, u, s] = np.eye(D2)
        at = 32 * cc + 9 * (u % 2)
        wp[at:at + D2, u // 2] = proj[:, rows].T
    for cc in range(GH):
        low = SLOT2 * cc + D2
        gb[low:low + D2, 0], gb[low:low + D2, 1] = -1, 1
        low = SLOT2 * cc + 2 * D2
        gb[low:low + D2, 2], gb[low:low + D2, 3] = -1, 1
    for cc in range(2):
        low = SLOT3 * cc + D3
        gb[low:low + D3, 4], gb[low:low + D3, 5] = -1, 1
        low = SLOT3 * cc + 2 * D3
        gb[low:low + D3, 6], gb[low:low + D3, 7] = -1, 1
    d["wq2"], d["wk2"], d["perm2"], d["wp2"], d["gb"] = (v.reshape(P, -1) for v in (wq, wk, perm, wp, gb))
    d["wv2"] = qkv[2 * D:].T
    d["row_bp2"] = f("L2_xattn_b_proj")[None]
    d["rt2"] = f("L2_ffn_router_w").T
    ex = np.stack([f("L2_ffn_w1_w").transpose(0, 2, 1), f("L2_ffn_wg_w").transpose(0, 2, 1),
                   f("L2_ffn_w2_w").reshape(NE, D, FT2, P).transpose(0, 3, 2, 1).reshape(NE, P, F2)], 2)
    d["experts"] = ex.reshape(NE, P, 3 * F2)
    d["bg2"] = f("L2_ffn_wg_b").reshape(NE * FT2, P).T
    d["b12"] = f("L2_ffn_w1_b").reshape(NE * FT2, P).T
    b2 = z(P, D)
    b2[:NE] = f("L2_ffn_w2_b")
    d["b2e"] = b2
    e = np.arange(NE)
    d["etri"] = np.broadcast_to((e[None, :] < e[:, None]).astype(np.float32).reshape(1, -1), (P, NE * NE))
    ws, wt, wo = f("L3_xattn_W_src"), f("L3_xattn_W_tgt"), f("L3_xattn_W_out")
    bs, bt = f("L3_xattn_b_src"), f("L3_xattn_b_tgt")
    wq, wk, bq, bk = z(P, 4, P), z(P, 2, 4, P), z(P, 4), z(P, 4)
    wo3 = z(P, 2, D)
    for h in range(H3):
        g, cc = h // 2, h % 2
        rows = slice(h * D3, (h + 1) * D3)
        for k in range(3):
            s = slice(SLOT3 * cc + k * D3, SLOT3 * cc + (k + 1) * D3)
            wq[:, g, s] = wt[rows].T
            wk[:, :, g, s] = ws[rows].T.reshape(2, P, D3).transpose(1, 0, 2)
            bq[s, g] = bt[rows]
            bk[s, g] = bs[rows]
        at = 32 * (h % GH)
        wo3[at:at + D3, h // GH] = wo[:, D + h * D3:D + (h + 1) * D3].T
    for cc in range(2):
        bq[SLOT3 * cc + MASKROW] = 1
        bk[SLOT3 * cc + MASKROW] = 1
    bk[MROW] = 1
    ms = z(P, 4)
    for cc in range(2):
        ms[SLOT3 * cc:SLOT3 * cc + 3 * D3, 0] = 1
        ms[SLOT3 * cc + MASKROW, 1] = 1
        ms[SLOT3 * cc + MASKROW, 3] = NEG
    ms[MROW, 2] = 1
    d["wq3"], d["wk3"], d["bq3"], d["bk3"], d["msel"], d["wo3"] = (v.reshape(P, -1) for v in (wq, wk, bq, bk, ms, wo3))
    d["wv3"] = ws[D:].T.reshape(2, P, D).transpose(1, 0, 2).reshape(P, -1)
    d["row_bv3"] = bs[None, D:]
    d["wox3"] = wo[:, :D].T
    d["row_bo3"] = f("L3_xattn_b_out")[None]
    d["rt3"], d["row_rb3"] = f("L3_ffn_router_w"), f("L3_ffn_router_b")[None]
    w1 = np.concatenate([f("L3_ffn_rw1"), f("L3_ffn_sw1")[None]])
    d["fw1"] = w1.transpose(1, 0, 2).reshape(P, -1)
    w2 = np.concatenate([f("L3_ffn_rw2"), f("L3_ffn_sw2")[None]])
    d["fw2"] = w2.reshape(E3, FT3, P, D).transpose(2, 0, 1, 3).reshape(P, -1)
    d["fb1"] = np.concatenate([f("L3_ffn_rb1"), f("L3_ffn_sb1")[None]]).reshape(E3 * FT3, P).T
    b2 = z(P, D)
    b2[:NE] = f("L3_ffn_rb2")
    d["fb2"], d["row_sb2"] = b2, f("L3_ffn_sb2")[None]
    return {k: np.ascontiguousarray(v) for k, v in d.items()}


STEPS = (84, 20)


def kernel(**inputs):
    import concourse.bacc as bacc
    from concourse.bass_utils import run_bass_kernel_spmd

    nc = bacc.Bacc("TRN2", target_bir_lowering=False, num_devices=1)
    arrays, t = {}, {}
    for name, a in layouts(inputs).items():
        arrays["in_" + name] = a
        t[name] = nc.dram_tensor("in_" + name, a.shape, mybir.dt.from_np(a.dtype), kind="ExternalInput").ap()
    t["out"] = nc.dram_tensor("out_0", (PAIRS, P, NT * D), F32, kind="ExternalOutput").ap()
    program(nc, t, STEPS)
    got = run_bass_kernel_spmd(nc, [arrays], core_ids=[0]).results[0]["out_0"]
    return got.reshape(PAIRS, P, 2, TT, D).transpose(0, 2, 3, 1, 4).reshape(B, T, D)
```
